# Optimizing a Trainium2 kernel written in Bass

```python
import numpy as np
import jax
import jax.numpy as jnp

def _softmax(x, axis=-1):
    return jax.nn.softmax(x, axis=axis)

def _gelu(x):
    return jax.nn.gelu(x, approximate=True)

def _silu(x):
    return jax.nn.silu(x)

def _sigmoid(x):
    return jax.nn.sigmoid(x)

def _layernorm(x, axis=-1, eps=1e-05):
    m = jnp.mean(x, axis=axis, keepdims=True)
    v = jnp.var(x, axis=axis, keepdims=True)
    return (x - m) / jnp.sqrt(v + eps)

def _scatter_add(tgt, idx, src, axis=0):
    return tgt.at[idx].add(src)

def _segment_sum(src, seg, n):
    return jax.ops.segment_sum(src, seg, n)
kernel_name = 'mk_xattn_ffn_d1_seqx_r4_23e59d'

def setup_inputs(seed: int=0):
    np.random.seed(seed)
    _w = jnp.asarray

    def _rec_inputs():
        import jax
        import jax.numpy as jnp
        _rk = jax.random.key(seed)
        x = 7.22e-05 + 1 * jax.random.normal(jax.random.fold_in(_rk, 1), (8, 256, 256), jnp.float32)
        _lenS = 256 - jax.random.randint(jax.random.fold_in(_rk, 7), (8,), 0, max(1, 256 // 4) + 1, jnp.int32)
        _lenS2 = 256 - jax.random.randint(jax.random.fold_in(_rk, 8), (8,), 0, max(1, 256 // 4) + 1, jnp.int32)
        _ctx_768P = jax.random.normal(jax.random.fold_in(_rk, 11), (8, 16, 192), jnp.float32)
        _ctx_768c = jax.random.dirichlet(jax.random.fold_in(_rk, 511), 0.3 * jnp.ones((16,), jnp.float32), (8, 256))
        _ctx_768t = jnp.einsum('bsk,bkd->bsd', _ctx_768c, _ctx_768P)
        _ctx_768t = _ctx_768t * jax.lax.rsqrt(jnp.mean(jnp.square(_ctx_768t)) + 1e-12) * 0.953939
        ctx_768 = -0.000191848 + 0.999787 * (_ctx_768t + 0.3 * jax.random.normal(jax.random.fold_in(_rk, 611), (8, 256, 192), jnp.float32))
        return (x, ctx_768)
    x, ctx_768 = _rec_inputs()

    def _L0_xattn_setup():
        import jax, jax.numpy as jnp
        import numpy as np
        DIM_Q = 256
        DIM_KV = 192
        N_HEADS = 4

        def _split_heads(x):
            b, l, d = x.shape
            return x.reshape(b, l, N_HEADS, d // N_HEADS).transpose(0, 2, 1, 3)
        key = jax.random.key(seed)
        ks = jax.random.split(key, 7)
        b, lq, lkv = (4, 512, 512)
        q = jax.random.normal(ks[0], (b, lq, DIM_Q), dtype=jnp.float32)
        kv = jax.random.normal(ks[1], (b, lkv, DIM_KV), dtype=jnp.float32)
        s_q = 1.0 / np.sqrt(DIM_Q)
        s_kv = 1.0 / np.sqrt(DIM_KV)
        Wq = jax.random.normal(ks[2], (DIM_Q, DIM_Q), dtype=jnp.float32) * s_q
        Wk = jax.random.normal(ks[3], (DIM_Q, DIM_KV), dtype=jnp.float32) * s_kv
        Wv = jax.random.normal(ks[4], (DIM_Q, DIM_KV), dtype=jnp.float32) * s_kv
        Wo = jax.random.normal(ks[5], (DIM_Q, DIM_Q), dtype=jnp.float32) * s_q
        bo = jax.random.normal(ks[6], (DIM_Q,), dtype=jnp.float32) * 0.01
        return {'q': q, 'kv': kv, 'Wq': Wq, 'Wk': Wk, 'Wv': Wv, 'Wo': Wo, 'bo': bo}
    _L0_xattn_all = _L0_xattn_setup()
    _L0_xattn_in = {k: v for k, v in _L0_xattn_all.items() if k in ('Wq', 'Wk', 'Wv', 'Wo', 'bo')}
    del _L0_xattn_all

    def _L0_ffn_setup():
        import jax, jax.numpy as jnp
        import numpy as np
        DIM = 256
        INTER = 128
        E = 32
        TOPK = 4
        GROUPS = 8
        TOPK_GROUPS = 4
        SHARED_INTER = 2 * INTER
        ROUTE_SCALE = 1.0
        B, S = (8, 1024)

        def _gate(xf, gw, gb):
            T = xf.shape[0]
            scores = jax.nn.softmax((xf @ gw + gb).astype(jnp.float32), axis=-1)
            original_scores = scores
            scores_g = scores.reshape(T, GROUPS, E // GROUPS)
            group_scores = jnp.sum(jax.lax.top_k(scores_g, 2)[0], axis=-1)
            gidx = jax.lax.top_k(group_scores, TOPK_GROUPS)[1]
            keep = jnp.zeros((T, GROUPS), bool).at[jnp.arange(T)[:, None], gidx].set(True)
            masked = jnp.where(keep[:, :, None], scores_g, -jnp.inf).reshape(T, E)
            indices = jax.lax.top_k(masked, TOPK)[1]
            weights = jnp.take_along_axis(original_scores, indices, axis=1) * ROUTE_SCALE
            return (weights.astype(xf.dtype), indices)
        key = jax.random.key(seed)
        ks = jax.random.split(key, 16)

        def xav(k, shape):
            fan_in, fan_out = (shape[-2], shape[-1])
            lim = np.sqrt(6.0 / (fan_in + fan_out))
            return jax.random.uniform(k, shape, jnp.float32, -lim, lim)
        return {'x': jax.random.normal(ks[0], (B, S, DIM), jnp.float32), 'gw': xav(ks[1], (DIM, E)), 'gb': jnp.zeros((E,), jnp.float32), 'w1': xav(ks[2], (E, DIM, INTER)), 'b1': jnp.zeros((E, INTER), jnp.float32), 'w3': xav(ks[3], (E, DIM, INTER)), 'b3': jnp.zeros((E, INTER), jnp.float32), 'w2': xav(ks[4], (E, INTER, DIM)), 'b2': jnp.zeros((E, DIM), jnp.float32), 'sw1': xav(ks[5], (DIM, SHARED_INTER)), 'sb1': jnp.zeros((SHARED_INTER,), jnp.float32), 'sw3': xav(ks[6], (DIM, SHARED_INTER)), 'sb3': jnp.zeros((SHARED_INTER,), jnp.float32), 'sw2': xav(ks[7], (SHARED_INTER, DIM)), 'sb2': jnp.zeros((DIM,), jnp.float32)}
    _L0_ffn_all = _L0_ffn_setup()
    _L0_ffn_in = {k: v for k, v in _L0_ffn_all.items() if k in ('gw', 'gb', 'w1', 'b1', 'w3', 'b3', 'w2', 'b2', 'sw1', 'sb1', 'sw3', 'sb3', 'sw2', 'sb2')}
    del _L0_ffn_all
    return {'x': x, 'ctx_768': ctx_768, 'L0_xattn_Wq': _L0_xattn_in['Wq'], 'L0_xattn_Wk': _L0_xattn_in['Wk'], 'L0_xattn_Wv': _L0_xattn_in['Wv'], 'L0_xattn_Wo': _L0_xattn_in['Wo'], 'L0_xattn_bo': _L0_xattn_in['bo'], 'L0_ffn_gw': _L0_ffn_in['gw'], 'L0_ffn_gb': _L0_ffn_in['gb'], 'L0_ffn_w1': _L0_ffn_in['w1'], 'L0_ffn_b1': _L0_ffn_in['b1'], 'L0_ffn_w3': _L0_ffn_in['w3'], 'L0_ffn_b3': _L0_ffn_in['b3'], 'L0_ffn_w2': _L0_ffn_in['w2'], 'L0_ffn_b2': _L0_ffn_in['b2'], 'L0_ffn_sw1': _L0_ffn_in['sw1'], 'L0_ffn_sb1': _L0_ffn_in['sb1'], 'L0_ffn_sw3': _L0_ffn_in['sw3'], 'L0_ffn_sb3': _L0_ffn_in['sb3'], 'L0_ffn_sw2': _L0_ffn_in['sw2'], 'L0_ffn_sb2': _L0_ffn_in['sb2']}

def reference(x, ctx_768, L0_xattn_Wq, L0_xattn_Wk, L0_xattn_Wv, L0_xattn_Wo, L0_xattn_bo, L0_ffn_gw, L0_ffn_gb, L0_ffn_w1, L0_ffn_b1, L0_ffn_w3, L0_ffn_b3, L0_ffn_w2, L0_ffn_b2, L0_ffn_sw1, L0_ffn_sb1, L0_ffn_sw3, L0_ffn_sb3, L0_ffn_sw2, L0_ffn_sb2):
    import jax
    import jax.numpy as jnp

    def _L0_xattn_ref(q, kv, Wq, Wk, Wv, Wo, bo):
        import jax, jax.numpy as jnp
        import numpy as np
        DIM_Q = 256
        DIM_KV = 192
        N_HEADS = 4

        def _split_heads(x):
            b, l, d = x.shape
            return x.reshape(b, l, N_HEADS, d // N_HEADS).transpose(0, 2, 1, 3)
        qp = q @ Wq.T
        kp = kv @ Wk.T
        vp = kv @ Wv.T
        qh, kh, vh = (_split_heads(qp), _split_heads(kp), _split_heads(vp))
        scale = (DIM_Q // N_HEADS) ** (-0.5)
        scores = jnp.einsum('bhqd,bhkd->bhqk', qh, kh) * scale
        attn = jax.nn.softmax(scores, axis=-1)
        ctx = jnp.einsum('bhqk,bhkd->bhqd', attn, vh)
        b, h, lq, hd = ctx.shape
        ctx = ctx.transpose(0, 2, 1, 3).reshape(b, lq, h * hd)
        return ctx @ Wo.T + bo

    def _L0_ffn_ref(x, gw, gb, w1, b1, w3, b3, w2, b2, sw1, sb1, sw3, sb3, sw2, sb2):
        import jax, jax.numpy as jnp
        import numpy as np
        DIM = 256
        INTER = 128
        E = 32
        TOPK = 4
        GROUPS = 8
        TOPK_GROUPS = 4
        SHARED_INTER = 2 * INTER
        ROUTE_SCALE = 1.0
        B, S = (8, 1024)

        def _gate(xf, gw, gb):
            T = xf.shape[0]
            scores = jax.nn.softmax((xf @ gw + gb).astype(jnp.float32), axis=-1)
            original_scores = scores
            scores_g = scores.reshape(T, GROUPS, E // GROUPS)
            group_scores = jnp.sum(jax.lax.top_k(scores_g, 2)[0], axis=-1)
            gidx = jax.lax.top_k(group_scores, TOPK_GROUPS)[1]
            keep = jnp.zeros((T, GROUPS), bool).at[jnp.arange(T)[:, None], gidx].set(True)
            masked = jnp.where(keep[:, :, None], scores_g, -jnp.inf).reshape(T, E)
            indices = jax.lax.top_k(masked, TOPK)[1]
            weights = jnp.take_along_axis(original_scores, indices, axis=1) * ROUTE_SCALE
            return (weights.astype(xf.dtype), indices)
        shape = x.shape
        xf = x.reshape(-1, DIM)
        T = xf.shape[0]
        weights, indices = _gate(xf, gw, gb)
        cw = jnp.zeros((T, E), xf.dtype).at[jnp.arange(T)[:, None], indices].add(weights)

        def body(y, p):
            w1e, b1e, w3e, b3e, w2e, b2e, we = p
            h = jax.nn.silu(xf @ w1e + b1e) * (xf @ w3e + b3e)
            return (y + we[:, None] * (h @ w2e + b2e), None)
        y0 = jnp.zeros_like(xf)
        y, _ = jax.lax.scan(body, y0, (w1, b1, w3, b3, w2, b2, cw.T))
        z = jax.nn.silu(xf @ sw1 + sb1) * (xf @ sw3 + sb3) @ sw2 + sb2
        return (y + z).reshape(shape)
    x = x + _L0_xattn_ref(_layernorm(x, axis=-1), ctx_768, L0_xattn_Wq, L0_xattn_Wk, L0_xattn_Wv, L0_xattn_Wo, L0_xattn_bo)
    x = x + _L0_ffn_ref(_layernorm(x, axis=-1), L0_ffn_gw, L0_ffn_gb, L0_ffn_w1, L0_ffn_b1, L0_ffn_w3, L0_ffn_b3, L0_ffn_w2, L0_ffn_b2, L0_ffn_sw1, L0_ffn_sb1, L0_ffn_sw3, L0_ffn_sb3, L0_ffn_sw2, L0_ffn_sb2)
    return x

_drawn_inputs = setup_inputs


def setup_inputs(seed=0):
    import zlib

    import numpy as np

    out = dict(_drawn_inputs(seed))
    spreads = {'L0_ffn_gb': (0.0, 0.321),
     'L0_ffn_b1': (0.0, 0.568),
     'L0_ffn_b3': (0.0, 0.586),
     'L0_ffn_b2': (0.0, 0.338),
     'L0_ffn_sb1': (0.0, 0.1),
     'L0_ffn_sb3': (0.0, 0.1),
     'L0_ffn_sb2': (0.0, 0.1)}
    factors = {'L0_xattn_bo': 4.341}
    for name, (base, spread) in spreads.items():
        noise = np.random.default_rng([zlib.crc32(name.encode()), seed]).standard_normal(out[name].shape)
        drawn = base * np.exp(spread * noise) if base else spread * noise
        out[name] = jnp.asarray(drawn.astype(out[name].dtype))
    for name, factor in factors.items():
        out[name] = (out[name] * factor).astype(out[name].dtype)
    return out
```

```python
from contextlib import ExitStack

import concourse.bass as bass
from concourse import mybir

F32 = mybir.dt.float32
BF16 = mybir.dt.bfloat16
I32 = mybir.dt.int32
U32 = mybir.dt.uint32
ALU = mybir.AluOpType
ACT = mybir.ActivationFunctionType
X = mybir.AxisListType.X

P = 128
BATCHES, LQ, D = 8, 256, 256
DKV = 192
HEADS, HD = 4, 64
TOKENS = BATCHES * LQ
TPB = LQ // P
TILES = TOKENS // P
KD = D // P
KC = DKV // 2
EXPERTS, INTER, TOPK = 32, 128, 4
GROUPS, GSIZE, TOPG = 8, 4, 4
SHARED = 2 * INTER
KS = SHARED // P
EPS = 1e-5
REGION = TOKENS + P
ROWS = EXPERTS * REGION + P
UNROLL = 6
SLOT_TILES = -(-((TOKENS * TOPK + EXPERTS * (P - 1)) // P) // UNROLL) * UNROLL
PAD = EXPERTS // 2
STEP_COUNT = 36
RING = 3


class Steps:

    def __init__(self, eng, sem):
        self.eng, self.sem, self.base, self.n, self.at = eng, sem, 0, 0, {}

    def body(self, base):
        self.base, self.n, self.at = base, 0, {}

    def did(self, ins, name):
        ins.then_inc(self.sem, 1)
        self.n += 1
        self.at[name] = self.n

    def count(self, name):
        return self.base + self.at[name]

    def need(self, name):
        self.eng.wait_ge(self.sem, self.count(name))


def spread(ap, axis, n):
    ap = ap.unsqueeze(axis)
    shape = list(ap.shape)
    shape[axis] = n
    return ap.to_broadcast(shape)


def run_slots(eng, slot):
    last = SLOT_TILES // UNROLL - 1
    slot(-1, UNROLL - 2, True, False, False)
    slot(-1, UNROLL - 1, True, False, False)
    for u in range(UNROLL):
        slot(0, u, True, True, u >= 1)
    with eng.Fori(1, last) as i:
        for u in range(UNROLL):
            slot(i, u, True, True, True)
    for u in range(UNROLL):
        slot(last, u, u < UNROLL - 2, True, True)
    slot(last + 1, 0, False, False, True)
    slot(last + 1, 1, False, False, False)


def build(nc, a, out):
    with ExitStack() as ctx:
        def sb(name, shape, dt=F32):
            return ctx.enter_context(nc.sbuf_tensor(name, shape, dt))

        def sem(name):
            return ctx.enter_context(nc.semaphore(name))

        dispatch = nc.dram_tensor("dispatch", [ROWS, D], F32, kind="Internal").ap()
        results = nc.dram_tensor("results", [SLOT_TILES * P, D], F32, kind="Internal").ap()

        w13 = sb("w13", [P, EXPERTS, KD, 2 * INTER])
        w2 = sb("w2", [P, EXPERTS, D])
        x = sb("x", [P, TILES, D])
        xn2T_all = sb("xn2T_all", [P, KD, TOKENS])
        sw13 = sb("sw13", [P, KD, 2 * SHARED])
        sw2 = sb("sw2", [P, KS, D])
        sb13 = sb("sb13", [P, 2 * KS])
        b2 = sb("b2", [EXPERTS + 1, D])
        gw = sb("gw", [P, KD, EXPERTS])
        gb = sb("gb", [P, EXPERTS])
        bo = sb("bo", [P, D])
        ident = sb("ident", [P, P])
        zeros = sb("zeros", [P, D])
        earlier = sb("earlier", [P, P], BF16)
        ones = sb("ones", [P, P], BF16)
        lower = sb("lower", [P, GROUPS, GROUPS])
        iota_e = sb("iota_e", [P, EXPERTS])
        region0 = sb("region0", [P, EXPERTS])
        iota_p = sb("iota_p", [P, 1])
        eps = sb("eps", [P, 1])
        cw = sb("cw", [P, TILES, EXPERTS + 1])
        wts = sb("wts", [P, TILES, TOPK])
        topf = sb("topf", [P, TILES, TOPK])
        rows_of = sb("rows_of", [P, TILES, TOPK])
        places_of = sb("places_of", [P, TILES, TOPK], U32)
        rstd1 = sb("rstd1", [P, TILES])
        nmr1 = sb("nmr1", [P, TILES])
        mv1 = sb("mv1", [P, TILES, 2])
        st1 = sb("st1", [P, TILES, 6])
        lnt1 = sb("lnt1", [P, 2, TILES])

        arena = sb("arena", [P, EXPERTS * 2 * INTER])
        at = [0]

        def part(*shape):
            n = 1
            for s in shape:
                n *= s
            v = arena[:, at[0]:at[0] + n]
            at[0] += n
            if len(shape) == 2:
                return v.rearrange("p (a b) -> p a b", a=shape[0])
            if len(shape) == 3:
                return v.rearrange("p (a b c) -> p a b c", a=shape[0], b=shape[1])
            if len(shape) == 4:
                return v.rearrange("p (a b c d) -> p a b c d", a=shape[0], b=shape[1], c=shape[2])
            return v

        xn = part(TPB, D)
        xnT = part(KD, LQ)
        qT = part(KD, LQ)
        kT = part(KD, LQ)
        v_sb = part(2, 2, D)
        probs = part(TPB, HEADS, LQ)
        pT = part(TPB, 2, HEADS, P)
        att = part(TPB, D)
        attT = part(TPB, KD, P)
        assert at[0] <= EXPERTS * 2 * INTER
        b13 = arena
        GR = 4
        got = arena[:, 0:GR * TOPK * D].rearrange("p (r k d) -> p r k d", r=GR, k=TOPK)

        work = sb("work", [P, 3840])
        wq = work[:, 0:512].rearrange("p (k n) -> p k n", k=KD)
        wk = work[:, 512:1024].rearrange("p (k n) -> p k n", k=KD)
        wv = work[:, 1024:1536].rearrange("p (k n) -> p k n", k=KD)
        wo = work[:, 1536:2048].rearrange("p (k n) -> p k n", k=KD)
        xn2 = work[:, 2048:3072].rearrange("p (a t d) -> p a t d", a=2, t=TPB)
        xn2T = work[:, 3072:3584].rearrange("p (k n) -> p k n", k=KD)
        e_x = work[:, 0:768].rearrange("p (r d) -> p r d", r=RING)
        e_xT = work[:, 768:1536].rearrange("p (r k s) -> p r k s", r=RING, k=KD)
        e_h = work[:, 1536:2048].rearrange("p (r n) -> p r n", r=2)
        e_g = work[:, 2048:2304].rearrange("p (r n) -> p r n", r=2)
        e_m = work[:, 2304:2560].rearrange("p (r n) -> p r n", r=2)
        e_mT = work[:, 2560:2816].rearrange("p (r n) -> p r n", r=2)
        e_y = work[:, 2816:3584].rearrange("p (r d) -> p r d", r=RING)

        hs_ctx = sb("hs_ctx", [P, 2 * 2 * LQ])
        ctx_now = hs_ctx[:, :].rearrange("p (a k n) -> p a k n", a=2, k=2)
        hs = hs_ctx[:, 0:KS * LQ].rearrange("p (k n) -> p k n", k=KS)
        cw_now = sb("cw_now", [P, TPB, EXPERTS + 1])
        cwT = sb("cwT", [EXPERTS + 1, TPB, P])
        nmax = sb("nmax", [P, TPB, HEADS])
        psums = sb("psums", [P, TPB, HEADS])
        prcp = sb("prcp", [P, TPB, HEADS])
        st2 = sb("st2", [P, TPB, 6])
        mv2 = sb("mv2", [P, TPB, 2])
        lnt2 = sb("lnt2", [P, 2, TPB])
        rstd2 = sb("rstd2", [P, TPB])
        logit = sb("logit", [P, TPB, EXPERTS])
        gmax = sb("gmax", [P, TPB])
        gexp = sb("gexp", [P, TPB, EXPERTS])
        gsum = sb("gsum", [P, TPB])
        score = sb("score", [P, TPB, EXPERTS])
        hi2 = sb("hi2", [P, TPB * GROUPS, 2])
        lo2 = sb("lo2", [P, TPB * GROUPS, 2])
        first = sb("first", [P, TPB * GROUPS])
        secnd = sb("secnd", [P, TPB * GROUPS])
        third = sb("third", [P, TPB * GROUPS])
        gscore = sb("gscore", [P, TPB, GROUPS])
        beats = sb("beats", [P, TPB, GROUPS, GROUPS])
        ties = sb("ties", [P, TPB, GROUPS, GROUPS])
        grank = sb("grank", [P, TPB, GROUPS])
        keep = sb("keep", [P, TPB, GROUPS])
        keep1 = sb("keep1", [P, TPB, GROUPS])
        masked = sb("masked", [P, TPB, EXPERTS])
        top = sb("top", [P, TPB, 8])
        topi = sb("topi", [P, TPB, 8], U32)
        onehot = sb("onehot", [P, TPB, TOPK, EXPERTS])
        picked = sb("picked", [P, TPB, TOPK, EXPERTS])
        chosen = sb("chosen", [P, TPB, EXPERTS], BF16)
        base = sb("base", [P, EXPERTS])
        rowof = sb("rowof", [P, TPB, EXPERTS])
        moved = sb("moved", [P, EXPERTS])
        shift = sb("shift", [P, TPB, TOPK])
        row_now = sb("row_now", [P, TPB, TOPK])
        slot_now = sb("slot_now", [P, 2, TPB * TOPK], U32)
        tail_row = sb("tail_row", [1, EXPERTS], I32)
        cnt = sb("cnt", [P, 3, PAD + EXPERTS])
        cnti = sb("cnti", [P, EXPERTS], I32)
        cols = sb("cols", [P, 4])
        table = sb("table", [1, 2, P], I32)
        gidx = sb("gidx", [P, GR, TOPK], U32)

        psS = ctx.enter_context(nc.psum_tensor("psS", [P, 4, 512], F32))
        psF = ctx.enter_context(nc.psum_tensor("psF", [P, 3, 512], F32))
        psG = ctx.enter_context(nc.psum_tensor("psG", [P, 512], F32))

        names = """x0_in xr_in wqkv_in wo_in gate_in bias_in shared_in w_in b13_in
            consts v_steps p_steps a_steps
            var1 lrstd1 norm1 xn_ready xnT_psum xnT_ready q_psum k_psum v_psum q_ready k_ready v_ready
            scores_psum nmax_ready probs_ready pT_psum pT_even pT_odd att_psum att_ready attT_psum
            attT_ready proj_psum res_ready x1_ready var2 lrstd2 xn2_ready xn2T_psum xn2T_ready xn2T_kept
            gate_psum gate_shifted gate_exp chosen_ready rank_psum rank_taken slots_ready
            table_cols table_psum table_ready tail_filled
            sh_psum sh_silu sh_ready cw_copied cwT_psum cwT_ready sh_out_psum sh_added
            exT_psum exT_ready eh_psum eh_ready eg_ready em_ready emT_psum emT_ready ey_psum ey_ready
            masked_ready placing places_ready weighed out_ready out_done""".split()
        s = {n: sem(n) for n in names}
        scattered = sem("scattered")
        ctx_in = [sem(f"ctx_in{i}") for i in range(2)]
        rows_in = [sem(f"rows_in{i}") for i in range(RING)]
        stored = [sem(f"stored{i}") for i in range(RING)]
        gathered = [sem(f"gathered{i}") for i in range(GR)]

        def wait_apart(eng, semaphore, value):
            eng.wait_ge(s["consts"], 1)
            eng.wait_ge(semaphore, value)

        top_ready = [sem(f"top_ready{j}") for j in range(TPB)]
        stats_ready = [sem(f"stats_ready{j}") for j in range(TPB)]
        gidx_first = sem("gidx_first")
        gidx_ready = [sem(f"gidx_ready{i}") for i in range(GR)]
        block = ctx.enter_context(nc.Block())
        ds = bass.ds
        LOOPS = (BATCHES - 2) // 2

        @block.sync
        def _(sp):
            xv = a["x"].rearrange("(t p) d -> p t d", p=P)
            sp.dma_start(x[:, 0:TPB, :], xv[:, 0:TPB, :]).then_inc(s["x0_in"], 16)
            sp.dma_start(x[:, TPB:, :], xv[:, TPB:, :]).then_inc(s["xr_in"], 16)
            sp.dma_start(wq, a["wq"]).then_inc(s["wqkv_in"], 16)
            sp.dma_start(wk[0:KC], a["wk"]).then_inc(s["wqkv_in"], 16)
            sp.dma_start(wv[0:KC], a["wv"]).then_inc(s["wqkv_in"], 16)
            for b in range(2):
                sp.dma_start(ctx_now[0:KC, b], a["ctxT"][:, :, b * LQ:(b + 1) * LQ]).then_inc(ctx_in[b], 16)
            sp.dma_start(wo, a["wo"]).then_inc(s["wo_in"], 16)
            sp.dma_start(gw[:, :, :], a["gw"]).then_inc(s["gate_in"], 16)
            sp.dma_start(gb[:, :], a["gb"].partition_broadcast(P)).then_inc(s["gate_in"], 16)
            sp.dma_start(bo[:, :], a["bo"].partition_broadcast(P)).then_inc(s["bias_in"], 16)
            sp.dma_start(sw13[:, :, :], a["sw13"]).then_inc(s["shared_in"], 16)
            sp.dma_start(sw2[:, :, :], a["sw2"]).then_inc(s["shared_in"], 16)
            sp.dma_start(sb13[:, :], a["sb13"]).then_inc(s["shared_in"], 16)
            sp.dma_start(b2[:, :], a["b2"]).then_inc(s["shared_in"], 16)
            EC = EXPERTS // BATCHES

            def expert_weights(b):
                sp.dma_start(w13[:, ds(b * EC, EC), :, :], a["w13"][:, ds(b * EC, EC), :, :]).then_inc(s["w_in"], 16)
                sp.dma_start(w2[:, ds(b * EC, EC), :], a["w2"][:, ds(b * EC, EC), :]).then_inc(s["w_in"], 16)

            expert_weights(0)
            expert_weights(1)
            with sp.Fori(1, BATCHES // 2) as i:
                for u in range(2):
                    sp.wait_ge(s["v_psum"], 2 * i + (u - 1))
                    sp.dma_start(ctx_now[0:KC, u], a["ctxT"][:, :, ds((2 * i + u) * LQ, LQ)]).then_inc(ctx_in[u], 16)
                    expert_weights(2 * i + u)
            sp.wait_ge(s["consts"], 1)
            sp.dma_start(dispatch[EXPERTS * REGION:ROWS, :], zeros[:, :]).then_inc(s["tail_filled"], 16)
            sp.wait_ge(s["proj_psum"], TILES)
            sp.wait_ge(s["x1_ready"], TILES)
            sp.dma_start(b13[:, :], a["b13"].partition_broadcast(P)).then_inc(s["b13_in"], 16)
            sp.wait_ge(s["table_ready"], 2)
            with sp.Fori(0, EXPERTS) as e:
                row = sp.value_load(tail_row[0:1, ds(e, 1)], min_val=0, max_val=ROWS - P)
                sp.dma_start(dispatch[ds(row, P), :], zeros[:, :]).then_inc(s["tail_filled"], 16)
            sp.wait_ge(s["tail_filled"], 16 * (EXPERTS + 1))
            sp.wait_ge(scattered, 16 * TPB * TOPK * BATCHES)

            def load(t, r, waits):
                if waits:
                    sp.wait_ge(s["exT_psum"], t - RING + 1)
                row = sp.value_load(table[0:1, 1, ds(t, 1)], min_val=0, max_val=ROWS - P)
                sp.dma_start(e_x[:, r, :], dispatch[ds(row, P), :]).then_inc(rows_in[r], 16)

            sp.wait_ge(s["sh_psum"], KS)
            for r in range(RING):
                load(r, r, False)
            with sp.Fori(1, SLOT_TILES // RING) as i:
                for r in range(RING):
                    load(i * RING + r, r, True)
            ov = out.rearrange("(t p) d -> p t d", p=P)
            with sp.Fori(0, TILES // GR) as i:
                for r in range(GR):
                    sp.wait_ge(s["out_ready"], i * GR + (r + 1))
                    sp.dma_start(ov[:, ds(i * GR + r, 1), :], x[:, ds(i * GR + r, 1), :]).then_inc(s["out_done"], 16)
            sp.wait_ge(s["out_done"], 16 * TILES)

        @block.gpsimd
        def _(pool):
            st = Steps(pool, s["p_steps"])
            pool.memset(zeros[:, :], 0.0).then_inc(s["consts"], 1)
            st.did(pool.memset(ident[:, :], 0.0), "ident0")
            st.did(pool.memset(earlier[:, :], 1.0), "earlier1")
            st.did(pool.memset(lower[:, :, :], 1.0), "lower1")
            pool.memset(ones[:, :], 1.0).then_inc(s["consts"], 1)
            pool.memset(eps[:, :], EPS).then_inc(s["consts"], 1)
            pool.memset(cw[:, :, EXPERTS:EXPERTS + 1], 1.0).then_inc(s["consts"], 1)
            st.need("ident0")
            pool.affine_select(out=ident[:, :], in_=ident[:, :], compare_op=ALU.not_equal, fill=1.0, base=0,
                               pattern=[[-1, P]], channel_multiplier=1).then_inc(s["consts"], 1)
            st.need("earlier1")
            pool.affine_select(out=earlier[:, :], in_=earlier[:, :], compare_op=ALU.is_gt, fill=0.0, base=0,
                               pattern=[[1, P]], channel_multiplier=-1).then_inc(s["consts"], 1)
            st.need("lower1")
            pool.affine_select(out=lower[:, :, :], in_=lower[:, :, :], compare_op=ALU.is_gt, fill=0.0, base=0,
                               pattern=[[1, GROUPS], [-1, GROUPS]], channel_multiplier=0).then_inc(s["consts"], 1)
            pool.iota(iota_e[:, :], pattern=[[1, EXPERTS]], base=0, channel_multiplier=0,
                      allow_small_or_imprecise_dtypes=True).then_inc(s["consts"], 1)
            pool.iota(region0[:, :], pattern=[[REGION, EXPERTS]], base=0, channel_multiplier=0,
                      allow_small_or_imprecise_dtypes=True).then_inc(s["consts"], 1)
            pool.iota(iota_p[:, :], pattern=[[0, 1]], base=0, channel_multiplier=1,
                      allow_small_or_imprecise_dtypes=True).then_inc(s["consts"], 1)
            pool.memset(work[:, 3072:3584], 0.0).then_inc(s["xn2T_kept"], 1)
            pool.wait_ge(s["bias_in"], 16)

            def residual(b):
                pool.wait_ge(s["xn_ready"], b + 1)
                pool.tensor_tensor(x[:, ds(TPB * b, TPB), :], x[:, ds(TPB * b, TPB), :],
                                   spread(bo[:, :], 1, TPB), ALU.add).then_inc(s["res_ready"], 1)

            def tail(b, par):
                pool.wait_ge(s["xn2T_ready"], b + 1)
                pool.tensor_copy(xn2T_all[:, :, ds(LQ * b, LQ)], xn2T).then_inc(s["xn2T_kept"], 1)
                wait_apart(pool, s["slots_ready"], b + 1)
                for j in range(TPB):
                    for k in range(TOPK):
                        pool.indirect_dma_start(
                            dispatch, bass.IndirectOffsetOnAxis(ap=slot_now[:, par, j * TOPK + k:j * TOPK + k + 1], axis=0),
                            xn2[:, par, j, :], None).then_inc(scattered, 16)
                pool.wait_ge(scattered, 16 * TPB * TOPK * (b + 1))

            residual(0)
            with pool.Fori(0, LOOPS) as i:
                for u in range(2):
                    residual(2 * i + (u + 1))
                    tail(2 * i + u, u)
            residual(BATCHES - 1)
            tail(BATCHES - 2, 0)
            tail(BATCHES - 1, 1)

            with pool.Fori(0, SLOT_TILES // RING) as i:
                for r in range(RING):
                    t = i * RING + r
                    pool.wait_ge(s["ey_ready"], t + 1)
                    pool.dma_start(results[ds(t * P, P), :], e_y[:, r, :]).then_inc(stored[r], 16)
            for r in range(RING):
                pool.wait_ge(stored[r], 16 * (SLOT_TILES // RING))

            pool.wait_ge(s["em_ready"], SLOT_TILES)

            pool.wait_ge(s["places_ready"], BATCHES)

            def gather(i, r):
                t = i * GR + r
                if not isinstance(i, int):
                    pool.wait_ge(s["out_ready"], t - GR + 1)
                copied = gidx_first if isinstance(i, int) else gidx_ready[r]
                pool.tensor_copy(gidx[:, r, :], places_of[:, ds(t, 1), :].rearrange("p a k -> p (a k)")).then_inc(copied, 1)
                if isinstance(i, int):
                    pool.wait_ge(copied, r + 1)
                else:
                    wait_apart(pool, copied, i)
                for k in range(TOPK):
                    pool.indirect_dma_start(got[:, r, k, :], None, results,
                                            bass.IndirectOffsetOnAxis(ap=gidx[:, r, k:k + 1], axis=0)).then_inc(gathered[r], 16)

            for r in range(GR):
                gather(0, r)
            with pool.Fori(1, TILES // GR) as i:
                for r in range(GR):
                    gather(i, r)

        @block.scalar
        def _(act):
            st = Steps(act, s["a_steps"])
            act.wait_ge(s["var1"], 1)
            act.wait_ge(s["consts"], 3)
            st.did(act.activation(lnt1[:, 0, :], mv1[:, :, 1], ACT.Ln, bias=eps[:, 0:1]), "ln1")
            st.need("ln1")
            act.activation(lnt1[:, 1, :], lnt1[:, 0, :], ACT.Exp, scale=-0.5).then_inc(s["lrstd1"], 1)
            act.wait_ge(s["norm1"], 1)

            def norm(b):
                if isinstance(b, int) and b == 0:
                    pass
                else:
                    act.wait_ge(s["xnT_psum"], b)
                for j in range(TPB):
                    ins = act.activation(xn[:, j, :], x[:, ds(TPB * b + j, 1), :].rearrange("p a d -> p (a d)"), ACT.Identity,
                                         scale=rstd1[:, ds(TPB * b + j, 1)], bias=nmr1[:, ds(TPB * b + j, 1)])
                ins.then_inc(s["xn_ready"], 1)

            def norm_out(b):
                act.wait_ge(s["xnT_psum"], b + 1)
                act.activation(xnT, psF[:, 2, :].rearrange("p (k n) -> p k n", k=KD), ACT.Copy).then_inc(s["xnT_ready"], 1)

            def qkv_out(b, par):
                act.wait_ge(s["q_psum"], b + 1)
                act.activation(qT, psF[:, 1, :].rearrange("p (k n) -> p k n", k=KD), ACT.Copy,
                               scale=float(HD) ** -0.5).then_inc(s["q_ready"], 1)
                act.wait_ge(s["k_psum"], b + 1)
                act.activation(kT, psF[:, 0, :].rearrange("p (k n) -> p k n", k=KD), ACT.Copy).then_inc(s["k_ready"], 1)
                act.wait_ge(s["v_psum"], b + 1)
                act.activation(v_sb[:, par], psF[:, 2, :].rearrange("p (k n) -> p k n", k=2), ACT.Copy).then_inc(s["v_ready"], 1)

            def exps(b, j):
                act.wait_ge(s["nmax_ready"], TPB * b + (j + 1))
                for hp in range(HEADS):
                    ins = act.activation(probs[:, j, hp, :], psS[:, 2 * j + hp // 2, (hp % 2) * LQ:(hp % 2 + 1) * LQ], ACT.Exp,
                                         bias=nmax[:, j, hp:hp + 1], accum_out=psums[:, j, hp:hp + 1])
                ins.then_inc(s["probs_ready"], 1)

            def gate_exps(b):
                act.wait_ge(s["gate_shifted"], b + 1)
                act.activation(gexp[:, :, :], logit[:, :, :], ACT.Exp).then_inc(s["gate_exp"], 1)

            def rest(b):
                for j in range(TPB):
                    act.wait_ge(s["pT_psum"], 2 * TPB * b + (2 * j + 1))
                    act.activation(pT[:, j, 0], psS[:, 2 * j, :].rearrange("p (h q) -> p h q", h=HEADS), ACT.Copy).then_inc(s["pT_even"], 1)
                for j in range(TPB):
                    act.wait_ge(s["attT_psum"], TPB * b + (j + 1))
                    act.activation(attT[:, j], psF[:, 2 - j, 0:D].rearrange("p (k q) -> p k q", k=KD), ACT.Copy).then_inc(s["attT_ready"], 1)
                act.wait_ge(s["var2"], b + 1)
                act.activation(lnt2[:, 0, :], mv2[:, :, 1], ACT.Ln, bias=eps[:, 0:1]).then_inc(s["a_steps"], 1)
                act.wait_ge(s["a_steps"], b + 2)
                act.activation(lnt2[:, 1, :], lnt2[:, 0, :], ACT.Exp, scale=-0.5).then_inc(s["lrstd2"], 1)

            def step(b, par, front, tail):
                if front:
                    norm(b + 1)
                    norm_out(b + 1)
                exps(b, 0)
                exps(b, 1)
                if tail:
                    gate_exps(b - 1)
                if front:
                    qkv_out(b + 1, 1 - par)
                rest(b)

            norm(0)
            norm_out(0)
            qkv_out(0, 0)
            step(0, 0, True, False)
            with act.Fori(0, LOOPS) as i:
                for u in range(2):
                    step(2 * i + (u + 1), 1 - u, True, True)
            step(BATCHES - 1, 1, False, True)
            gate_exps(BATCHES - 1)

            act.wait_ge(s["table_psum"], 1)
            act.activation(table[0:1, :, :], psG[0:1, 0:2 * P].rearrange("p (a t) -> p a t", a=2), ACT.Copy).then_inc(s["table_ready"], 1)

            def shared(c, after):
                if after:
                    act.wait_ge(s["cwT_psum"], c)
                act.activation(cw_now[:, :, :], cw[:, ds(TPB * c, TPB), :], ACT.Copy).then_inc(s["cw_copied"], 1)
                for m in range(KS):
                    act.wait_ge(s["sh_psum"], KS * c + (m + 1))
                    act.activation(hs[:, m, :], psS[:, 2 * m, 0:LQ], ACT.Silu, bias=sb13[:, m:m + 1]).then_inc(s["sh_silu"], 1)
                act.wait_ge(s["cwT_psum"], c + 1)
                act.activation(cwT[:, :, :], psF[0:EXPERTS + 1, 2, 0:LQ].rearrange("p (t q) -> p t q", t=TPB), ACT.Copy).then_inc(s["cwT_ready"], 1)

            def experts(i, u, ahead, now, back):
                t = i * UNROLL + u
                if ahead:
                    act.wait_ge(s["exT_psum"], t + 3)
                    act.activation(e_xT[:, (u + 2) % RING], psS[:, u % 2, 0:D].rearrange("p (k q) -> p k q", k=KD), ACT.Copy).then_inc(s["exT_ready"], 1)
                if now:
                    act.wait_ge(s["eh_ready"], t + 1)
                    act.activation(e_g[:, u % 2, :], e_h[:, u % 2, 0:INTER], ACT.Silu).then_inc(s["eg_ready"], 1)
                if back:
                    act.wait_ge(s["emT_psum"], t)
                    act.activation(e_mT[:, (u + 1) % 2, :], psF[:, (u + 1) % 2, 0:P], ACT.Copy).then_inc(s["emT_ready"], 1)

            act.wait_ge(s["chosen_ready"], BATCHES)
            shared(0, False)
            with act.Fori(1, 4) as c:
                shared(c, True)
            run_slots(act, experts)
            with act.Fori(4, BATCHES) as c:
                shared(c, True)

        @block.tensor
        def _(pe):
            pe.wait_ge(s["consts"], 5)

            def norm_T(b):
                pe.wait_ge(s["xn_ready"], b + 1)
                for j in range(TPB):
                    for k in range(KD):
                        ins = pe.transpose(psF[:, 2, k * LQ + j * P:k * LQ + (j + 1) * P], xn[:, j, k * P:(k + 1) * P], ident[:, :])
                ins.then_inc(s["xnT_psum"], 1)

            def proj_q(b):
                pe.wait_ge(s["xnT_ready"], b + 1)
                if not isinstance(b, int) or b >= 2:
                    pe.wait_ge(s["x1_ready"], TPB * (b - 1))
                for m in range(KD):
                    for k in range(KD):
                        ins = pe.matmul(psF[:, 1, m * LQ:(m + 1) * LQ], wq[:, k, m * P:(m + 1) * P], xnT[:, k, :],
                                        start=(k == 0), stop=(k == KD - 1))
                ins.then_inc(s["q_psum"], 1)

            def proj_k(b, par, nth):
                pe.wait_ge(ctx_in[par], 16 * nth)
                for m in range(KD):
                    for k in range(2):
                        ins = pe.matmul(psF[:, 0, m * LQ:(m + 1) * LQ], wk[0:KC, k, m * P:(m + 1) * P],
                                        ctx_now[0:KC, par, k, :], start=(k == 0), stop=(k == 1))
                ins.then_inc(s["k_psum"], 1)

            def proj_v(b, par):
                for t in range(2):
                    for k in range(2):
                        ins = pe.matmul(psF[:, 2, t * D:(t + 1) * D], ctx_now[0:KC, par, k, t * P:(t + 1) * P], wv[0:KC, k, :],
                                        start=(k == 0), stop=(k == 1))
                ins.then_inc(s["v_psum"], 1)

            def scores(b, j):
                if j == 0:
                    pe.wait_ge(s["q_ready"], b + 1)
                    pe.wait_ge(s["k_ready"], b + 1)
                for h in range(HEADS):
                    r = HD * (h % 2)
                    ins = pe.matmul(psS[:, 2 * j + h % 2, (h // 2) * LQ:(h // 2 + 1) * LQ], qT[r:r + HD, h // 2, j * P:(j + 1) * P],
                                    kT[r:r + HD, h // 2, :], start=True, stop=True)
                ins.then_inc(s["scores_psum"], 1)

            def probs_T(b, j):
                pe.wait_ge(s["probs_ready"], TPB * b + (j + 1))
                for t in range(2):
                    for hp in range(HEADS):
                        ins = pe.transpose(psS[:, 2 * j + t, hp * P:(hp + 1) * P], probs[:, j, hp, t * P:(t + 1) * P], ident[:, :])
                    ins.then_inc(s["pT_psum"], 1)

            def attend(b, j, par, front):
                pe.wait_ge(s["pT_even"], TPB * b + (j + 1))
                pe.wait_ge(s["pT_odd"], TPB * b + (j + 1))
                pe.wait_ge(s["v_ready"], b + 1)
                if front:
                    pe.wait_ge(s["q_ready" if j == 0 else "k_ready"], b + 2)
                for hp in range(HEADS):
                    h = (hp % 2) * 2 + hp // 2
                    for t in range(2):
                        ins = pe.matmul(psF[:, 1 - j, h * HD:(h + 1) * HD], pT[:, j, t, hp, :], v_sb[:, par, t, h * HD:(h + 1) * HD],
                                        start=(t == 0), stop=(t == 1))
                ins.then_inc(s["att_psum"], 1)

            def attend_T(b, j, front):
                pe.wait_ge(s["att_ready"], TPB * b + (j + 1))
                if front and j == 0:
                    pe.wait_ge(s["v_ready"], b + 2)
                for k in range(KD):
                    ins = pe.transpose(psF[:, 2 - j, k * P:(k + 1) * P], att[:, j, k * P:(k + 1) * P], ident[:, :])
                ins.then_inc(s["attT_psum"], 1)

            def project(b, j):
                pe.wait_ge(s["attT_ready"], TPB * b + (j + 1))
                for k in range(KD):
                    ins = pe.matmul(psF[:, j, 0:D], attT[:, j, k, :], wo[:, k, :], start=(k == 0), stop=(k == KD - 1))
                ins.then_inc(s["proj_psum"], 1)

            def norm2_T(b, par):
                pe.wait_ge(s["xn2_ready"], b + 1)
                if not isinstance(b, int) or b >= 1:
                    pe.wait_ge(s["rank_taken"], b + 1)
                for j in range(TPB):
                    for k in range(KD):
                        ins = pe.transpose(psG[:, k * LQ + j * P:k * LQ + (j + 1) * P], xn2[:, par, j, k * P:(k + 1) * P], ident[:, :])
                ins.then_inc(s["xn2T_psum"], 1)

            def gate(b):
                pe.wait_ge(s["xn2T_ready"], b + 1)
                for j in range(TPB):
                    for k in range(KD):
                        ins = pe.matmul(psG[:, j * EXPERTS:(j + 1) * EXPERTS], xn2T[:, k, j * P:(j + 1) * P], gw[:, k, :],
                                        start=(k == 0), stop=(k == KD - 1))
                ins.then_inc(s["gate_psum"], 1)

            def ranks(b):
                pe.wait_ge(s["chosen_ready"], b + 1)
                pe.matmul(psG[:, 0:32], earlier[:, :], chosen[:, 0, :], start=True, stop=True)
                pe.matmul(psG[:, 32:64], earlier[:, :], chosen[:, 1, :], start=True, stop=False)
                pe.matmul(psG[:, 32:64], ones[:, :], chosen[:, 0, :], start=False, stop=True)
                pe.matmul(psG[:, 64:96], ones[:, :], chosen[:, 0, :], start=True, stop=False)
                pe.matmul(psG[:, 64:96], ones[:, :], chosen[:, 1, :], start=False, stop=True).then_inc(s["rank_psum"], 1)

            def step(b, par, front, tail, nth):
                scores(b, 0)
                if front:
                    norm_T(b + 1)
                scores(b, 1)
                if tail:
                    norm2_T(b - 1, 1 - par)
                if front:
                    proj_q(b + 1)
                if tail:
                    gate(b - 1)
                if front:
                    proj_k(b + 1, 1 - par, nth)
                    proj_v(b + 1, 1 - par)
                probs_T(b, 0)
                probs_T(b, 1)
                attend(b, 0, par, front)
                attend(b, 1, par, front)
                if tail:
                    ranks(b - 1)
                attend_T(b, 0, front)
                attend_T(b, 1, front)
                project(b, 0)
                project(b, 1)

            norm_T(0)
            pe.wait_ge(s["wqkv_in"], 48)
            proj_q(0)
            proj_k(0, 0, 1)
            proj_v(0, 0)
            pe.wait_ge(s["wo_in"], 16)
            pe.wait_ge(s["gate_in"], 32)
            step(0, 0, True, False, 1)
            with pe.Fori(0, LOOPS) as i:
                for u in range(2):
                    step(2 * i + (u + 1), 1 - u, True, True, i + 2)
            step(BATCHES - 1, 1, False, True, None)
            norm2_T(BATCHES - 1, 1)
            gate(BATCHES - 1)
            ranks(BATCHES - 1)
            pe.wait_ge(s["table_cols"], 2)
            for n in range(2):
                ins = pe.matmul(psG[0:1, n * P:(n + 1) * P], cols[:, n:n + 1], ident[:, :], start=True, stop=True)
            ins.then_inc(s["table_psum"], 1)
            pe.wait_ge(s["shared_in"], 64)
            pe.wait_ge(s["xn2T_kept"], BATCHES + 1)

            def shared(c, after):
                pe.wait_ge(s["cw_copied"], c + 1)
                if after:
                    pe.wait_ge(s["sh_ready"], KS * c)
                for m in range(KS):
                    for n in range(2):
                        for k in range(KD):
                            ins = pe.matmul(psS[:, 2 * m + n, 0:LQ], sw13[:, k, n * SHARED + m * P:n * SHARED + (m + 1) * P],
                                            xn2T_all[:, k, ds(c * LQ, LQ)], start=(k == 0), stop=(k == KD - 1))
                    ins.then_inc(s["sh_psum"], 1)
                for j in range(TPB):
                    ins = pe.transpose(psF[0:EXPERTS + 1, 2, j * P:(j + 1) * P], cw_now[:, j, :], ident[:, :])
                ins.then_inc(s["cwT_psum"], 1)
                pe.wait_ge(s["sh_ready"], KS * c + KS)
                pe.wait_ge(s["cwT_ready"], c + 1)
                for j in range(TPB):
                    if after:
                        pe.wait_ge(s["sh_added"], TPB * c + (j - 1))
                    for m in range(KS):
                        pe.matmul(psF[:, j, 0:D], hs[:, m, j * P:(j + 1) * P], sw2[:, m, :], start=(m == 0), stop=False)
                    pe.matmul(psF[:, j, 0:D], cwT[:, j, :], b2[:, :], start=False, stop=True).then_inc(s["sh_out_psum"], 1)

            def expert_of(t):
                return pe.value_load(table[0:1, 0, ds(t, 1)], min_val=0, max_val=EXPERTS - 1)

            def experts(i, u, ahead, now, back):
                t = i * UNROLL + u
                if now:
                    e = expert_of(t)
                    pe.wait_ge(s["exT_ready"], t + 1)
                    if not isinstance(t, int) or t >= 2:
                        pe.wait_ge(s["eh_ready"], t - 1)
                    for k in range(KD):
                        ins = pe.matmul(psS[:, 2 + u % 2, 0:2 * INTER], e_xT[:, u % RING, k, :],
                                        w13[:, ds(e, 1), k, :].rearrange("p a n -> p (a n)"), start=(k == 0), stop=(k == KD - 1))
                    ins.then_inc(s["eh_psum"], 1)
                if ahead:
                    n = (u + 2) % RING
                    pe.wait_ge(rows_in[n], 16 * (i * (UNROLL // RING) + ((u + 2) // RING + 1)))
                    for k in range(KD):
                        ins = pe.transpose(psS[:, u % 2, k * P:(k + 1) * P], e_x[:, n, k * P:(k + 1) * P], ident[:, :])
                    ins.then_inc(s["exT_psum"], 1)
                if back:
                    pe.wait_ge(s["em_ready"], t)
                    pe.transpose(psF[:, (u + 1) % 2, 0:P], e_m[:, (u + 1) % 2, :], ident[:, :]).then_inc(s["emT_psum"], 1)
                if not isinstance(t, int) or 2 <= t:
                    e = expert_of(t - 2)
                    pe.wait_ge(s["emT_ready"], t - 1)
                    if not isinstance(t, int) or t >= 4:
                        pe.wait_ge(s["ey_ready"], t - 3)
                    bank = psF[:, 2, 0:D] if u % 2 == 0 else psG[:, 0:D]
                    pe.matmul(bank, e_mT[:, u % 2, :], w2[:, ds(e, 1), :].rearrange("p a n -> p (a n)"),
                              start=True, stop=True).then_inc(s["ey_psum"], 1)

            shared(0, False)
            with pe.Fori(1, 4) as c:
                shared(c, True)
            pe.wait_ge(s["table_ready"], 2)
            pe.wait_ge(s["w_in"], 16 * 2 * BATCHES)
            pe.wait_ge(s["sh_added"], TPB * 4)
            run_slots(pe, experts)
            pe.wait_ge(s["ey_ready"], SLOT_TILES)
            with pe.Fori(4, BATCHES) as c:
                shared(c, True)

        @block.vector
        def _(dve):
            st = Steps(dve, s["v_steps"])

            def newton(dst, rough, var, tmp, n):
                st.did(dve.scalar_tensor_tensor(tmp, var, EPS, rough, ALU.add, ALU.mult), n + "vy")
                st.need(n + "vy")
                st.did(dve.tensor_tensor(tmp, tmp, rough, ALU.mult), n + "vyy")
                st.need(n + "vyy")
                st.did(dve.tensor_scalar(tmp, tmp, -0.5, 1.5, ALU.mult, ALU.add), n + "half")
                st.need(n + "half")
                st.did(dve.tensor_tensor(dst, rough, tmp, ALU.mult), n + "rstd")

            for t in range(TILES):
                if t == 0:
                    dve.wait_ge(s["x0_in"], 16)
                if t == TPB:
                    dve.wait_ge(s["xr_in"], 16)
                st.did(dve.bn_stats(st1[:, t, :], x[:, t, :]), f"stats{t}")
            for t in range(TILES):
                st.need(f"stats{t}")
                ins = dve.bn_aggr(mv1[:, t, :], st1[:, t, :])
            ins.then_inc(s["var1"], 1)
            dve.wait_ge(s["lrstd1"], 1)
            newton(rstd1[:, :], lnt1[:, 1, :], mv1[:, :, 1], lnt1[:, 0, :], "n1")
            st.need("n1rstd")
            dve.scalar_tensor_tensor(nmr1[:, :], mv1[:, :, 0], -1.0, rstd1[:, :], ALU.mult, ALU.mult).then_inc(s["norm1"], 1)
            dve.wait_ge(s["consts"], 10)
            dve.wait_ge(s["gate_in"], 32)
            dve.tensor_copy(base[:, :], region0[:, :]).then_inc(s["rank_taken"], 1)
            start = st.n

            def maxima(b, j):
                dve.wait_ge(s["scores_psum"], TPB * b + (j + 1))
                dve.tensor_reduce(nmax[:, j, :], psS[:, 2 * j:2 * j + 2, :].rearrange("p a (c n) -> p a c n", c=2), X, ALU.max,
                                  negate=True).then_inc(s["nmax_ready"], 1)

            def norm2_out(b):
                dve.wait_ge(s["xn2T_psum"], b + 1)
                dve.wait_ge(s["xn2T_kept"], b + 1)
                dve.tensor_copy(xn2T, psG[:, :].rearrange("p (k n) -> p k n", k=KD)).then_inc(s["xn2T_ready"], 1)

            def gate_shift(b):
                dve.wait_ge(s["gate_psum"], b + 1)
                st.did(dve.tensor_tensor(logit[:, :, :], psG[:, 0:TPB * EXPERTS].rearrange("p (t e) -> p t e", t=TPB),
                                         spread(gb[:, :], 1, TPB), ALU.add), "logit")
                st.need("logit")
                st.did(dve.tensor_reduce(gmax[:, :], logit[:, :, :], X, ALU.max), "gmax")
                st.need("gmax")
                dve.tensor_tensor(logit[:, :, :], logit[:, :, :], spread(gmax[:, :], 2, EXPERTS), ALU.subtract).then_inc(s["gate_shifted"], 1)

            def route_groups(b):
                dve.wait_ge(s["gate_exp"], b + 1)
                st.did(dve.tensor_reduce(gsum[:, :], gexp[:, :, :], X, ALU.add), "gsum")
                st.need("gsum")
                st.did(dve.reciprocal(gsum[:, :], gsum[:, :]), "grcp")
                st.need("grcp")
                st.did(dve.tensor_tensor(score[:, :, :], gexp[:, :, :], spread(gsum[:, :], 2, EXPERTS), ALU.mult), "score")
                st.need("score")
                sv = score[:, :, :].rearrange("p t (g c) -> p (t g) c", c=GSIZE)
                st.did(dve.tensor_tensor(hi2[:, :, :], sv[:, :, 0:2], sv[:, :, 2:4], ALU.max), "hi2")
                st.did(dve.tensor_tensor(lo2[:, :, :], sv[:, :, 0:2], sv[:, :, 2:4], ALU.min), "lo2")
                st.need("hi2")
                st.did(dve.tensor_tensor(first[:, :], hi2[:, :, 0], hi2[:, :, 1], ALU.max), "first")
                st.did(dve.tensor_tensor(secnd[:, :], hi2[:, :, 0], hi2[:, :, 1], ALU.min), "secnd")
                st.need("lo2")
                st.did(dve.tensor_tensor(third[:, :], lo2[:, :, 0], lo2[:, :, 1], ALU.max), "third")
                st.need("third")
                st.did(dve.tensor_tensor(secnd[:, :], secnd[:, :], third[:, :], ALU.max), "second")
                st.need("second")
                st.did(dve.tensor_tensor(gscore[:, :, :].rearrange("p t g -> p (t g)"), first[:, :], secnd[:, :], ALU.add), "gscore")
                st.need("gscore")
                other, own = spread(gscore[:, :, :], 2, GROUPS), spread(gscore[:, :, :], 3, GROUPS)
                st.did(dve.tensor_tensor(ties[:, :, :, :], other, own, ALU.is_equal), "equal")
                st.did(dve.tensor_tensor(beats[:, :, :, :], other, own, ALU.is_gt), "beats")
                st.need("equal")
                st.did(dve.tensor_tensor(ties[:, :, :, :].rearrange("p t g h -> p t (g h)"), ties[:, :, :, :].rearrange("p t g h -> p t (g h)"),
                                         spread(lower[:, :, :].rearrange("p g h -> p (g h)"), 1, TPB), ALU.mult), "ties")
                st.need("ties")
                st.did(dve.tensor_tensor(beats[:, :, :, :], beats[:, :, :, :], ties[:, :, :, :], ALU.add), "ahead")
                st.need("ahead")
                st.did(dve.tensor_reduce(grank[:, :, :], beats[:, :, :, :], X, ALU.add), "grank")
                st.need("grank")
                st.did(dve.tensor_scalar(keep[:, :, :], grank[:, :, :], TOPG - 0.5, None, ALU.is_lt), "keep")
                st.did(dve.tensor_scalar(keep1[:, :, :], grank[:, :, :], TOPG - 0.5, 1.0, ALU.is_lt, ALU.subtract), "keep1")

            def route_experts(b):
                sv = score[:, :, :].rearrange("p t (g c) -> p (t g) c", c=GSIZE)
                mv = masked[:, :, :].rearrange("p t (g c) -> p (t g) c", c=GSIZE)
                kv, k1 = (z[:, :, :].rearrange("p t g -> p (t g)") for z in (keep, keep1))
                st.need("keep1")
                st.did(dve.tensor_tensor(mv, sv, spread(kv, 2, GSIZE), ALU.mult), "kept")
                st.need("kept")
                dve.tensor_tensor(mv, mv, spread(k1, 2, GSIZE), ALU.add).then_inc(s["masked_ready"], 1)
                wait_apart(dve, s["masked_ready"], b + 1)
                for j in range(TPB):
                    dve.max(top[:, j, :], masked[:, j, :]).then_inc(top_ready[j], 1)
                for j in range(TPB):
                    wait_apart(dve, top_ready[j], b + 1)
                    st.did(dve.max_index(topi[:, j, :], top[:, j, :], masked[:, j, :]), f"topi{j}")
                st.need(f"topi{TPB - 1}")
                st.did(dve.tensor_copy(topf[:, ds(TPB * b, TPB), :], topi[:, :, 0:TOPK]), "topf")
                st.need("topf")
                st.did(dve.tensor_tensor(onehot[:, :, :, :].rearrange("p t k e -> p (t k) e"), spread(iota_e[:, :], 1, TPB * TOPK),
                                         spread(topf[:, ds(TPB * b, TPB), :].rearrange("p t k -> p (t k)"), 2, EXPERTS), ALU.is_equal), "onehot")
                st.need("onehot")
                with nc.allow_low_precision("zeros and ones"):
                    ins = dve.tensor_reduce(chosen[:, :, :], onehot[:, :, :, :].rearrange("p t k e -> p t e k"), X, ALU.add)
                st.did(ins, "chosen")
                st.need("chosen")
                dve.tensor_tensor(cw[:, ds(TPB * b, TPB), 0:EXPERTS], score[:, :, :], chosen[:, :, :], ALU.mult).then_inc(s["chosen_ready"], 1)
                st.did(dve.tensor_copy(wts[:, ds(TPB * b, TPB), :], top[:, :, 0:TOPK]), "wts")

            def rank_take(b, par):
                dve.wait_ge(s["rank_psum"], b + 1)
                dve.wait_ge(s["rank_taken"], b + 1)
                st.did(dve.tensor_tensor(rowof[:, :, :], psG[:, 0:TPB * EXPERTS].rearrange("p (t e) -> p t e", t=TPB),
                                         spread(base[:, :], 1, TPB), ALU.add), "rowof")
                st.need("rowof")
                dve.tensor_tensor(base[:, :], psG[:, 64:64 + EXPERTS], base[:, :], ALU.add).then_inc(s["rank_taken"], 1)
                for j in range(TPB):
                    ins = dve.tensor_tensor(picked[:, j], onehot[:, j], spread(rowof[:, j, :], 1, TOPK), ALU.mult)
                    st.did(ins, f"picked{j}")
                st.need(f"picked{TPB - 1}")
                st.did(dve.tensor_reduce(row_now[:, :, :], picked[:, :, :, :], X, ALU.add), "rows_of")
                st.need("rows_of")
                dve.tensor_copy(slot_now[:, par, :], row_now[:, :, :].rearrange("p t k -> p (t k)")).then_inc(s["slots_ready"], 1)
                st.did(dve.tensor_copy(rows_of[:, ds(TPB * b, TPB), :], row_now[:, :, :]), "kept_rows")

            def probs_out(b):
                for j in range(TPB):
                    dve.wait_ge(s["pT_psum"], 2 * TPB * b + (2 * j + 2))
                    dve.tensor_copy(pT[:, j, 1], psS[:, 2 * j + 1, :].rearrange("p (h q) -> p h q", h=HEADS)).then_inc(s["pT_odd"], 1)

            def attend_out(b):
                dve.wait_ge(s["probs_ready"], TPB * b + 2)
                st.did(dve.reciprocal(prcp[:, :, :], psums[:, :, :]), "prcp")
                st.need("prcp")
                for j in range(TPB):
                    dve.wait_ge(s["att_psum"], TPB * b + (j + 1))
                    dve.tensor_tensor(att[:, j, :].rearrange("p (h l d) -> p l h d", l=2, d=HD),
                                      psF[:, 1 - j, 0:D].rearrange("p (h l d) -> p l h d", l=2, d=HD),
                                      spread(prcp[:, j, :].rearrange("p (l h) -> p l h", l=2), 3, HD), ALU.mult).then_inc(s["att_ready"], 1)

            def residual(b, par):
                dve.wait_ge(s["res_ready"], b + 1)
                for j in range(TPB):
                    xt = x[:, ds(TPB * b + j, 1), :].rearrange("p a d -> p (a d)")
                    dve.wait_ge(s["proj_psum"], TPB * b + (j + 1))
                    dve.tensor_tensor(xt, psF[:, j, 0:D], xt, ALU.add).then_inc(s["x1_ready"], 1)
                for j in range(TPB):
                    xt = x[:, ds(TPB * b + j, 1), :].rearrange("p a d -> p (a d)")
                    wait_apart(dve, s["x1_ready"], TPB * b + (j + 1))
                    dve.bn_stats(st2[:, j, :], xt).then_inc(stats_ready[j], 1)
                for j in range(TPB):
                    wait_apart(dve, stats_ready[j], b + 1)
                    ins = dve.bn_aggr(mv2[:, j, :], st2[:, j, :])
                ins.then_inc(s["var2"], 1)
                dve.wait_ge(s["lrstd2"], b + 1)
                newton(rstd2[:, :], lnt2[:, 1, :], mv2[:, :, 1], lnt2[:, 0, :], "n2")
                st.need("n2rstd")
                for j in range(TPB):
                    xt = x[:, ds(TPB * b + j, 1), :].rearrange("p a d -> p (a d)")
                    ins = dve.tensor_scalar(xn2[:, par, j, :], xt, mv2[:, j, 0:1], rstd2[:, j:j + 1], ALU.subtract, ALU.mult)
                ins.then_inc(s["xn2_ready"], 1)

            def step(b, par, tail):
                maxima(b, 0)
                maxima(b, 1)
                if tail:
                    norm2_out(b - 1)
                    gate_shift(b - 1)
                    route_groups(b - 1)
                probs_out(b)
                if tail:
                    route_experts(b - 1)
                attend_out(b)
                if tail:
                    rank_take(b - 1, 1 - par)
                residual(b, par)

            st.body(start)
            step(0, 0, False)
            n0 = start + st.n
            with dve.Fori(0, LOOPS) as i:
                for u in range(2):
                    pb = n0 + (i * (2 * STEP_COUNT) + u * STEP_COUNT)
                    st.body(pb)
                    step(2 * i + (u + 1), 1 - u, True)
                    assert st.n == STEP_COUNT, st.n
            n1 = n0 + 2 * LOOPS * STEP_COUNT
            st.body(n1)
            step(BATCHES - 1, 1, True)
            b = BATCHES - 1
            norm2_out(b)
            gate_shift(b)
            route_groups(b)
            route_experts(b)
            rank_take(b, 1)

            dve.wait_ge(s["rank_taken"], BATCHES + 1)
            dve.tensor_copy(tail_row[:, :], base[0:1, :]).then_inc(s["table_ready"], 1)
            st.did(dve.memset(cnt[:, :, :], 0.0), "cnt0")
            st.did(dve.scalar_tensor_tensor(cnti[:, :], base[:, :], float(P - 1), region0[:, :], ALU.add, ALU.subtract), "tokens")
            st.need("tokens")
            st.did(dve.tensor_scalar(cnti[:, :], cnti[:, :], P.bit_length() - 1, None, ALU.arith_shift_right), "tiles")
            st.need("tiles")
            st.need("cnt0")
            st.did(dve.tensor_copy(cnt[:, 0, PAD:], cnti[:, :]), "prefix0")
            k, cur, n = 1, 0, 0
            while k < EXPERTS:
                st.need(f"prefix{n}")
                n += 1
                st.did(dve.tensor_tensor(cnt[:, 1 - cur, PAD:], cnt[:, cur, PAD:], cnt[:, cur, PAD - k:PAD + EXPERTS - k], ALU.add), f"prefix{n}")
                k, cur = 2 * k, 1 - cur
            ends, before, start_t = cnt[:, cur, PAD:], cnt[:, 1 - cur, PAD:], cnt[:, 2, 0:1]
            st.need(f"prefix{n}")
            st.did(dve.tensor_scalar(before, ends, iota_p[:, 0:1], None, ALU.is_le), "before")
            st.need("before")
            st.did(dve.tensor_reduce(cols[:, 2:3], before, X, ALU.add), "expert")
            st.did(dve.tensor_tensor(before, before, ends, ALU.mult), "ended")
            st.need("ended")
            st.did(dve.tensor_reduce(start_t, before, X, ALU.max), "start")
            st.need("start")
            st.did(dve.tensor_tensor(start_t, iota_p[:, 0:1], start_t, ALU.subtract), "nth")
            st.did(dve.tensor_scalar(cols[:, 3:4], cols[:, 2:3], EXPERTS - 0.5, float(P), ALU.is_lt, ALU.mult), "rows")
            st.need("rows")
            st.did(dve.tensor_tensor(start_t, start_t, cols[:, 3:4], ALU.mult), "into")
            st.need("into")
            dve.tensor_scalar(cols[:, 0:1], cols[:, 2:3], EXPERTS - 1.0, None, ALU.min).then_inc(s["table_cols"], 1)
            dve.scalar_tensor_tensor(cols[:, 1:2], cols[:, 2:3], float(REGION), start_t, ALU.mult, ALU.add).then_inc(s["table_cols"], 1)
            st.did(dve.scalar_tensor_tensor(moved[:, :], cnt[:, cur, PAD - 1:PAD - 1 + EXPERTS], float(P), region0[:, :],
                                            ALU.mult, ALU.subtract), "moved")
            st.need("moved")

            def places(c):
                dve.tensor_tensor(onehot[:, :, :, :].rearrange("p t k e -> p (t k) e"), spread(iota_e[:, :], 1, TPB * TOPK),
                                  spread(topf[:, ds(TPB * c, TPB), :].rearrange("p t k -> p (t k)"), 2, EXPERTS),
                                  ALU.is_equal).then_inc(s["placing"], 1)
                dve.wait_ge(s["placing"], 3 * c + 1)
                dve.tensor_tensor(picked[:, :, :, :].rearrange("p t k e -> p (t k) e"), onehot[:, :, :, :].rearrange("p t k e -> p (t k) e"),
                                  spread(moved[:, :], 1, TPB * TOPK), ALU.mult).then_inc(s["placing"], 1)
                dve.wait_ge(s["placing"], 3 * c + 2)
                dve.tensor_reduce(shift[:, :, :], picked[:, :, :, :], X, ALU.add).then_inc(s["placing"], 1)
                dve.wait_ge(s["placing"], 3 * c + 3)
                dve.tensor_tensor(places_of[:, ds(TPB * c, TPB), :], rows_of[:, ds(TPB * c, TPB), :], shift[:, :, :],
                                  ALU.add).then_inc(s["places_ready"], 1)

            def shared(c):
                for m in range(KS):
                    dve.wait_ge(s["sh_silu"], KS * c + (m + 1))
                    dve.scalar_tensor_tensor(hs[:, m, :], psS[:, 2 * m + 1, 0:LQ], sb13[:, KS + m:KS + m + 1], hs[:, m, :],
                                             ALU.add, ALU.mult).then_inc(s["sh_ready"], 1)
                for j in range(TPB):
                    xt = x[:, ds(TPB * c + j, 1), :].rearrange("p a d -> p (a d)")
                    dve.wait_ge(s["sh_out_psum"], TPB * c + (j + 1))
                    dve.tensor_tensor(xt, psF[:, j, 0:D], xt, ALU.add).then_inc(s["sh_added"], 1)

            def experts(i, u, ahead, now, back):
                t = i * UNROLL + u
                if now:
                    e = dve.value_load(table[0:1, 0, ds(t, 1)], min_val=0, max_val=EXPERTS - 1)
                    dve.wait_ge(s["eh_psum"], t + 1)
                    dve.tensor_tensor(e_h[:, u % 2, :], psS[:, 2 + u % 2, 0:2 * INTER], b13[:, ds(e * (2 * INTER), 2 * INTER)],
                                      ALU.add).then_inc(s["eh_ready"], 1)
                if not isinstance(t, int) or t >= 2:
                    r = (u + RING - 2) % RING
                    dve.wait_ge(s["ey_psum"], t - 1)
                    if not isinstance(t, int) or t - 2 >= RING:
                        dve.wait_ge(stored[r], 16 * (i * (UNROLL // RING) + (u - 2) // RING))
                    bank = psF[:, 2, 0:D] if u % 2 == 0 else psG[:, 0:D]
                    dve.tensor_copy(e_y[:, r, :], bank).then_inc(s["ey_ready"], 1)
                if now:
                    dve.wait_ge(s["eg_ready"], t + 1)
                    dve.tensor_tensor(e_m[:, u % 2, :], e_g[:, u % 2, :], e_h[:, u % 2, INTER:], ALU.mult).then_inc(s["em_ready"], 1)

            with dve.Fori(0, 4) as c:
                shared(c)
                for u in range(2):
                    places(2 * c + u)
            dve.wait_ge(s["table_ready"], 2)
            dve.wait_ge(s["b13_in"], 16)
            run_slots(dve, experts)
            with dve.Fori(4, BATCHES) as c:
                shared(c)

            with dve.Fori(0, TILES // GR) as i:
                for r in range(GR):
                    t = i * GR + r
                    xt = x[:, ds(t, 1), :].rearrange("p a d -> p (a d)")
                    dve.wait_ge(gathered[r], 16 * TOPK * (i + 1))
                    for k in range(TOPK):
                        w = wts[:, ds(t, 1), k:k + 1].rearrange("p a k -> p (a k)")
                        ins = dve.scalar_tensor_tensor(xt, got[:, r, k, :], w, xt, ALU.mult, ALU.add)
                        if k < TOPK - 1:
                            ins.then_inc(s["weighed"], 1)
                            dve.wait_ge(s["weighed"], (TOPK - 1) * t + (k + 1))
                    ins.then_inc(s["out_ready"], 1)


_OUT = (BATCHES, LQ, D)


def _halves(w):
    return w.reshape(2, w.shape[0] // 2, -1).transpose(1, 0, 2)


def kernel(**inputs):
    import numpy as np
    import concourse.bacc as bacc
    from concourse import mybir as mb
    from concourse.bass_utils import run_bass_kernel_spmd

    g = {n: np.asarray(v) for n, v in inputs.items()}
    f = {n[len("L0_ffn_"):]: v for n, v in g.items() if n.startswith("L0_ffn_")}
    t = {n[len("L0_xattn_"):]: v for n, v in g.items() if n.startswith("L0_xattn_")}
    w13 = np.concatenate([f["w1"], f["w3"]], axis=2)
    laid = {
        "x": g["x"].reshape(TOKENS, D),
        "ctxT": _halves(g["ctx_768"].reshape(TOKENS, DKV).T),
        "wq": _halves(t["Wq"].T), "wk": _halves(t["Wk"].T), "wv": _halves(t["Wv"].T), "wo": _halves(t["Wo"].T),
        "bo": t["bo"], "gw": _halves(f["gw"]), "gb": f["gb"],
        "w13": w13.reshape(EXPERTS, KD, P, 2 * INTER).transpose(2, 0, 1, 3),
        "w2": f["w2"].transpose(1, 0, 2),
        "b13": np.concatenate([f["b1"], f["b3"]], axis=1).reshape(-1),
        "b2": np.concatenate([f["b2"], f["sb2"][None]], axis=0),
        "sw13": _halves(np.concatenate([f["sw1"], f["sw3"]], axis=1)),
        "sw2": _halves(f["sw2"]),
        "sb13": np.concatenate([f["sb1"], f["sb3"]]).reshape(2 * KS, P).T,
    }
    laid = {n: np.ascontiguousarray(v) for n, v in laid.items()}
    nc = bacc.Bacc("TRN2", target_bir_lowering=False, num_devices=1)
    aps = {n: nc.dram_tensor(f"in_{n}", v.shape, mb.dt.from_np(v.dtype), kind="ExternalInput").ap() for n, v in laid.items()}
    out = nc.dram_tensor("out", [TOKENS, D], F32, kind="ExternalOutput").ap()
    build(nc, aps, out)
    r = run_bass_kernel_spmd(nc, [{f"in_{n}": v for n, v in laid.items()}], core_ids=[0])
    return r.results[0]["out"].reshape(_OUT)
```

```python
from contextlib import ExitStack

import concourse.bass as bass
from concourse import mybir

F32 = mybir.dt.float32
BF16 = mybir.dt.bfloat16
I32 = mybir.dt.int32
U32 = mybir.dt.uint32
ALU = mybir.AluOpType
ACT = mybir.ActivationFunctionType
X = mybir.AxisListType.X

P = 128
BATCHES, LQ, D = 8, 256, 256
DKV = 192
HEADS, HD = 4, 64
TOKENS = BATCHES * LQ
TPB = LQ // P
TILES = TOKENS // P
KD = D // P
KC = DKV // 2
EXPERTS, INTER, TOPK = 32, 128, 4
GROUPS, GSIZE, TOPG = 8, 4, 4
SHARED = 2 * INTER
KS = SHARED // P
EPS = 1e-5
REGION = TOKENS + P
DISPATCH_ROWS = EXPERTS * REGION + P
ROW = D + EXPERTS + 1
UNROLL = 6
SLOT_TILES = -(-((TOKENS * TOPK + EXPERTS * (P - 1)) // P) // UNROLL) * UNROLL
LAST = SLOT_TILES // UNROLL - 1
OUT_ROWS = TOKENS + P
TAILS = 8
PAD = EXPERTS // 2
STEP_COUNT = 43
RSQRT_MAGIC = 0x5F3759DF


class Steps:

    def __init__(self, eng, sem):
        self.eng, self.sem, self.base, self.n, self.at = eng, sem, 0, 0, {}

    def body(self, base):
        self.base, self.n, self.at = base, 0, {}

    def did(self, ins, name):
        ins.then_inc(self.sem, 1)
        self.n += 1
        self.at[name] = self.n

    def count(self, name):
        return self.base + self.at[name]

    def need(self, name):
        self.eng.wait_ge(self.sem, self.count(name))


def spread(ap, axis, n):
    ap = ap.unsqueeze(axis)
    shape = list(ap.shape)
    shape[axis] = n
    return ap.to_broadcast(shape)


def run_slots(eng, slot, begin=lambda i: None):
    begin(0)
    for u in range(-2, UNROLL):
        slot(0, u)
    with eng.Fori(1, LAST) as i:
        begin(i)
        for u in range(UNROLL):
            slot(i, u)
    begin(LAST)
    for u in range(UNROLL + 3):
        slot(LAST, u)


def values(eng, regs, row, last):
    eng.load(regs, row)
    return [eng.snap(r, min_val=0, max_val=last) for r in regs]


class TileExperts:

    def __init__(self, eng, table):
        self.eng, self.table, self.e = eng, table, None
        self.regs = [eng.alloc_register(f"expert{n}") for n in range(UNROLL + 3)]

    def begin(self, i):
        skip = 3 if isinstance(i, int) and i == 0 else 0
        row = self.table[0:1, 0, bass.ds(i * UNROLL + (skip - 3), UNROLL + 3 - skip)]
        self.e = [None] * skip + values(self.eng, self.regs[skip:], row, EXPERTS - 1)

    def of(self, u, d):
        return self.e[u + d + 3]


def lies(i, u, d):
    return not isinstance(i, int) or 0 <= i * UNROLL + u + d < SLOT_TILES


def ring(i, u, d):
    return i * UNROLL + (u + d), (u + d) % UNROLL, i + (u + d) // UNROLL


def build(nc, a, out):
    with ExitStack() as ctx:
        def sb(name, shape, dt=F32):
            return ctx.enter_context(nc.sbuf_tensor(name, shape, dt))

        def sem(name):
            return ctx.enter_context(nc.semaphore(name))

        dispatch = nc.dram_tensor("dispatch", [DISPATCH_ROWS, ROW], F32, kind="Internal").ap()
        odd_sums = nc.dram_tensor("odd_sums", [OUT_ROWS, D], F32, kind="Internal").ap()
        sums = (out, odd_sums)

        w13 = sb("w13", [P, EXPERTS, KD, 2 * INTER])
        w2 = sb("w2", [P, EXPERTS, D])
        x = sb("x", [P, TILES, D])
        xn2T_all = sb("xn2T_all", [P, BATCHES, KD, LQ])
        sw13 = sb("sw13", [P, KD, 2 * SHARED])
        sw2 = sb("sw2", [P, KS, D])
        sb13 = sb("sb13", [P, 2 * KS])
        b2 = sb("b2", [EXPERTS + 1, D])
        gw = sb("gw", [P, KD, EXPERTS])
        gb = sb("gb", [P, EXPERTS])
        bo = sb("bo", [P, D])
        ident = sb("ident", [P, P])
        padding = sb("padding", [P, ROW])
        no_sums = sb("no_sums", [P, D])
        token = sb("token", [P, TILES])
        earlier = sb("earlier", [P, P], BF16)
        ones = sb("ones", [P, P], BF16)
        lower = sb("lower", [P, GROUPS, GROUPS])
        iota_e = sb("iota_e", [P, EXPERTS])
        region0 = sb("region0", [P, EXPERTS])
        iota_p = sb("iota_p", [P, 1])
        zero1 = sb("zero1", [P, 1], U32)
        cw = sb("cw", [P, TILES, EXPERTS + 1])
        rstd1 = sb("rstd1", [P, TILES])
        nmr1 = sb("nmr1", [P, TILES])
        mv1 = sb("mv1", [P, TILES, 2])
        st1 = sb("st1", [P, TILES, 6])
        rsq = sb("rsq", [P, 2, TILES])

        arena = sb("arena", [P, EXPERTS * 2 * INTER])
        at = [0]

        def part(*shape):
            n = 1
            for s in shape:
                n *= s
            v = arena[:, at[0]:at[0] + n]
            at[0] += n
            if len(shape) == 2:
                return v.rearrange("p (a b) -> p a b", a=shape[0])
            if len(shape) == 3:
                return v.rearrange("p (a b c) -> p a b c", a=shape[0], b=shape[1])
            if len(shape) == 4:
                return v.rearrange("p (a b c d) -> p a b c d", a=shape[0], b=shape[1], c=shape[2])
            return v

        xn = part(TPB, D)
        xnT = part(KD, LQ)
        qT = part(KD, LQ)
        kT = part(KD, LQ)
        v_sb = part(2, 2, D)
        probs = part(TPB, HEADS, LQ)
        pT = part(TPB, 2, HEADS, P)
        att = part(TPB, D)
        attT = part(TPB, KD, P)
        assert at[0] <= EXPERTS * 2 * INTER
        b13 = arena

        work = sb("work", [P, 4 * KD * D + 2 * TPB * ROW + KD * LQ])
        wq = work[:, 0:512].rearrange("p (k n) -> p k n", k=KD)
        wk = work[:, 512:1024].rearrange("p (k n) -> p k n", k=KD)
        wv = work[:, 1024:1536].rearrange("p (k n) -> p k n", k=KD)
        wo = work[:, 1536:2048].rearrange("p (k n) -> p k n", k=KD)
        n = 2048 + 2 * TPB * ROW
        xn2 = work[:, 2048:n].rearrange("p (a t d) -> p a t d", a=2, t=TPB)
        xn2T = work[:, n:n + KD * LQ].rearrange("p (k n) -> p k n", k=KD)
        e_xT = work[:, 0:768].rearrange("p (r k s) -> p r k s", r=3, k=KD)
        e_h = work[:, 768:1280].rearrange("p (r n) -> p r n", r=2)
        e_g = work[:, 1280:1536].rearrange("p (r n) -> p r n", r=2)
        e_m = work[:, 1536:1792].rearrange("p (r n) -> p r n", r=2)
        e_mT = work[:, 1792:2048].rearrange("p (r n) -> p r n", r=2)
        e_meta = work[:, 2048:2048 + UNROLL * EXPERTS].rearrange("p (r n) -> p r n", r=UNROLL)
        shared_in = xn2T_all[:, :, :, :].rearrange("p b k n -> p (b k n)")
        e_x = shared_in[:, 0:UNROLL * ROW].rearrange("p (r d) -> p r d", r=UNROLL)
        E_X_CHUNKS = -(-UNROLL * ROW // (KD * LQ))
        n = E_X_CHUNKS * KD * LQ
        e_y = shared_in[:, n:n + UNROLL * D].rearrange("p (r d) -> p r d", r=UNROLL)

        hs_ctx = sb("hs_ctx", [P, 2 * 2 * LQ])
        ctx_now = hs_ctx[:, :].rearrange("p (a k n) -> p a k n", a=2, k=2)
        hs = hs_ctx[:, :].rearrange("p (a k n) -> p a k n", a=2, k=KS)
        cw_now = sb("cw_now", [P, TPB, EXPERTS + 1])
        cwT = sb("cwT", [EXPERTS + 1, TPB, P])
        nmax = sb("nmax", [P, TPB, HEADS])
        psums = sb("psums", [P, TPB, HEADS])
        prcp = sb("prcp", [P, TPB, HEADS])
        st2 = sb("st2", [P, TPB, 6])
        mv2 = sb("mv2", [P, TPB, 2])
        rstd2 = sb("rstd2", [P, TPB])
        logit = sb("logit", [P, TPB, EXPERTS])
        gmax = sb("gmax", [P, TPB])
        gexp = sb("gexp", [P, TPB, EXPERTS])
        gsum = sb("gsum", [P, TPB])
        score = sb("score", [P, TPB, EXPERTS])
        hi2 = sb("hi2", [P, TPB * GROUPS, 2])
        lo2 = sb("lo2", [P, TPB * GROUPS, 2])
        first = sb("first", [P, TPB * GROUPS])
        secnd = sb("secnd", [P, TPB * GROUPS])
        third = sb("third", [P, TPB * GROUPS])
        gscore = sb("gscore", [P, TPB, GROUPS])
        beats = sb("beats", [P, TPB, GROUPS, GROUPS])
        ties = sb("ties", [P, TPB, GROUPS, GROUPS])
        grank = sb("grank", [P, TPB, GROUPS])
        keep = sb("keep", [P, TPB, GROUPS])
        keep1 = sb("keep1", [P, TPB, GROUPS])
        masked = sb("masked", [P, TPB, EXPERTS])
        top = sb("top", [P, TPB, 8])
        topi = sb("topi", [P, TPB, 8], U32)
        topf = sb("topf", [P, TPB, TOPK])
        onehot = sb("onehot", [P, TPB, TOPK, EXPERTS])
        picked = sb("picked", [P, TPB, TOPK, EXPERTS])
        chosen = sb("chosen", [P, TPB, EXPERTS], BF16)
        base = sb("base", [P, EXPERTS])
        rowof = sb("rowof", [P, TPB, EXPERTS])
        row_now = sb("row_now", [P, TPB, TOPK])
        slot_now = sb("slot_now", [P, 2, TPB * TOPK], U32)
        tail_row = sb("tail_row", [1, EXPERTS], I32)
        cnt = sb("cnt", [P, 3, PAD + EXPERTS])
        cnti = sb("cnti", [P, EXPERTS], I32)
        cols = sb("cols", [P, 4])
        table = sb("table", [1, 2, P], I32)
        e_number = sb("e_number", [P, UNROLL], U32)
        e_token = sb("e_token", [P, UNROLL], U32)

        psS = ctx.enter_context(nc.psum_tensor("psS", [P, 4, 512], F32))
        psF = ctx.enter_context(nc.psum_tensor("psF", [P, 3, 512], F32))
        psG = ctx.enter_context(nc.psum_tensor("psG", [P, 512], F32))

        names = """x0_in x1_in xr_in wk_in wv_in wq_in wo_in gate_in bias_in shared_in w_in b13_in
            consts v_steps p_steps padding_ready
            norm1 xn_ready xnT_psum xnT_ready q_psum k_psum v_psum q_ready k_ready v_ready
            scores_psum nmax_ready probs_ready pT_psum pT_ready att_psum att_ready attT_psum
            attT_ready proj_psum res_ready x1_ready xn2_ready xn2T_psum xn2T_ready xn2T_kept
            gate_psum gate_shifted gate_exp masked_ready chosen_ready rank_psum rank_taken slots_ready
            cw_kept copy_ready table_cols table_psum tail_rows table_ready dump_filled tail_filled
            sh_psum sh_silu sh_ready cw_copied cwT_psum cwT_ready sh_out_psum sh_added
            x2_stored sums_cleared
            exT_psum exT_ready eh_psum eh_ready eg_ready em_ready emT_psum emT_ready ey_psum
            meta_copied out_done""".split()
        s = {n: sem(n) for n in names}
        scattered = sem("scattered")
        ctx_in = [sem(f"ctx_in{i}") for i in range(2)]
        top_ready = [sem(f"top_ready{j}") for j in range(TPB)]
        stats_ready = [sem(f"stats_ready{j}") for j in range(TPB)]
        rows_in = [sem(f"rows_in{r}") for r in range(UNROLL)]
        ey_ready = [sem(f"ey_ready{r}") for r in range(UNROLL)]
        token_ready = [sem(f"token_ready{r}") for r in range(UNROLL)]
        added = [sem(f"added{r}") for r in range(UNROLL)]
        first_added = [sem(f"first_added{r}") for r in range(UNROLL - 2)]
        CONSTS = 14

        def wait_apart(eng, semaphore, value):
            eng.wait_ge(s["consts"], 1)
            eng.wait_ge(semaphore, value)

        def shared_bank(c, m):
            return psF[:, m, :] if c == 0 else psS[:, 2 * (c % 2) + m, :]

        block = ctx.enter_context(nc.Block())
        ds = bass.ds
        MID = (2, BATCHES - 2)

        @block.sync
        def _(sp):
            xv = a["x"].rearrange("(t p) d -> p t d", p=P)

            def context(b, par):
                sp.dma_start(ctx_now[0:KC, par], a["ctxT"][:, :, ds(b * LQ, LQ)]).then_inc(ctx_in[par], 16)

            sp.dma_start(x[:, 0:TPB, :], xv[:, 0:TPB, :]).then_inc(s["x0_in"], 16)
            context(0, 0)
            sp.dma_start(wk[0:KC], a["wk"]).then_inc(s["wk_in"], 16)
            sp.dma_start(wv[0:KC], a["wv"]).then_inc(s["wv_in"], 16)
            sp.dma_start(wq, a["wq"]).then_inc(s["wq_in"], 16)
            sp.dma_start(x[:, TPB:2 * TPB, :], xv[:, TPB:2 * TPB, :]).then_inc(s["x1_in"], 16)
            sp.dma_start(x[:, 2 * TPB:, :], xv[:, 2 * TPB:, :]).then_inc(s["xr_in"], 16)
            context(1, 1)
            sp.dma_start(bo[:, :], a["bo"].partition_broadcast(P)).then_inc(s["bias_in"], 16)
            sp.dma_start(wo, a["wo"]).then_inc(s["wo_in"], 16)
            sp.dma_start(gw[:, :, :], a["gw"]).then_inc(s["gate_in"], 16)
            sp.dma_start(gb[:, :], a["gb"].partition_broadcast(P)).then_inc(s["gate_in"], 16)
            sp.dma_start(sw13[:, :, :], a["sw13"]).then_inc(s["shared_in"], 16)
            sp.dma_start(sw2[:, :, :], a["sw2"]).then_inc(s["shared_in"], 16)
            sp.dma_start(sb13[:, :], a["sb13"]).then_inc(s["shared_in"], 16)
            sp.dma_start(b2[:, :], a["b2"]).then_inc(s["shared_in"], 16)
            EC = EXPERTS // BATCHES

            def expert_weights(b):
                sp.dma_start(w13[:, ds(b * EC, EC), :, :], a["w13"][:, ds(b * EC, EC), :, :]).then_inc(s["w_in"], 16)
                sp.dma_start(w2[:, ds(b * EC, EC), :], a["w2"][:, ds(b * EC, EC), :]).then_inc(s["w_in"], 16)

            expert_weights(0)
            expert_weights(1)
            with sp.Fori(1, BATCHES // 2) as i:
                for u in range(2):
                    sp.wait_ge(s["v_psum"], 2 * i + (u - 1))
                    context(2 * i + u, u)
                    expert_weights(2 * i + u)
            sp.wait_ge(s["padding_ready"], 3)
            sp.dma_start(dispatch[EXPERTS * REGION:, :], padding[:, :]).then_inc(s["dump_filled"], 16)
            sp.dma_start(out[TOKENS:, :], no_sums[:, :]).then_inc(s["sums_cleared"], 16)
            sp.dma_start(odd_sums.rearrange("(t p) d -> p t d", p=P), spread(no_sums[:, :], 1, OUT_ROWS // P)).then_inc(s["sums_cleared"], 16)
            sp.wait_ge(s["proj_psum"], BATCHES)
            sp.dma_start(b13[:, :], a["b13"].partition_broadcast(P)).then_inc(s["b13_in"], 16)
            sp.wait_ge(s["tail_rows"], 1)
            tail_regs = [sp.alloc_register(f"tail{n}") for n in range(TAILS)]
            with sp.Fori(0, EXPERTS // TAILS) as i:
                for row in values(sp, tail_regs, tail_row[0:1, ds(i * TAILS, TAILS)], DISPATCH_ROWS - P):
                    sp.dma_start(dispatch[ds(row, P), :], padding[:, :]).then_inc(s["tail_filled"], 16)

            sp.wait_ge(s["dump_filled"], 16)
            sp.wait_ge(s["tail_filled"], 16 * EXPERTS)
            sp.wait_ge(scattered, 16 * TPB * TOPK * BATCHES)
            sp.wait_ge(s["sh_psum"], KS * E_X_CHUNKS)
            sp.wait_ge(s["table_ready"], 1)
            row_regs = [sp.alloc_register(f"row{r}") for r in range(UNROLL)]

            def load(i):
                rows = values(sp, row_regs, table[0:1, 1, ds(i * UNROLL, UNROLL)], DISPATCH_ROWS - P)
                for r in range(UNROLL):
                    if not isinstance(i, int):
                        sp.wait_ge(s["meta_copied"], i * UNROLL + (r - UNROLL + 1))
                    sp.dma_start(e_x[:, r, :], dispatch[ds(rows[r], P), :]).then_inc(rows_in[r], 16)

            load(0)
            ov = out[0:TOKENS, :].rearrange("(t p) d -> p t d", p=P)
            with sp.Fori(0, BATCHES) as c:
                sp.wait_ge(s["sh_added"], c + 1)
                sp.dma_start(ov[:, ds(TPB * c, TPB), :], x[:, ds(TPB * c, TPB), :]).then_inc(s["x2_stored"], 16)
            with sp.Fori(1, SLOT_TILES // UNROLL) as i:
                load(i)
            sp.wait_ge(s["x2_stored"], 16 * BATCHES)
            sp.wait_ge(s["sums_cleared"], 32)

        @block.gpsimd
        def _(pool):
            st = Steps(pool, s["p_steps"])
            st.did(pool.memset(ident[:, :], 0.0), "ident0")
            st.did(pool.memset(earlier[:, :], 1.0), "earlier1")
            st.did(pool.memset(lower[:, :, :], 1.0), "lower1")
            st.need("ident0")
            pool.affine_select(out=ident[:, :], in_=ident[:, :], compare_op=ALU.not_equal, fill=1.0, base=0,
                               pattern=[[-1, P]], channel_multiplier=1).then_inc(s["consts"], 1)
            st.need("earlier1")
            pool.affine_select(out=earlier[:, :], in_=earlier[:, :], compare_op=ALU.is_gt, fill=0.0, base=0,
                               pattern=[[1, P]], channel_multiplier=-1).then_inc(s["consts"], 1)
            st.need("lower1")
            pool.affine_select(out=lower[:, :, :], in_=lower[:, :, :], compare_op=ALU.is_gt, fill=0.0, base=0,
                               pattern=[[1, GROUPS], [-1, GROUPS]], channel_multiplier=0).then_inc(s["consts"], 1)
            pool.memset(ones[:, :], 1.0).then_inc(s["consts"], 1)
            pool.memset(cw[:, :, EXPERTS:EXPERTS + 1], 1.0).then_inc(s["consts"], 1)
            pool.memset(zero1[:, :], 0).then_inc(s["consts"], 1)

            def count(dst, pattern, base, step):
                return pool.iota(dst, pattern=pattern, base=base, channel_multiplier=step, allow_small_or_imprecise_dtypes=True)

            count(iota_e[:, :], [[1, EXPERTS]], 0, 0).then_inc(s["consts"], 1)
            count(region0[:, :], [[REGION, EXPERTS]], 0, 0).then_inc(s["consts"], 1)
            count(iota_p[:, :], [[0, 1]], 0, 1).then_inc(s["consts"], 1)
            count(token[:, :], [[P, TILES]], 0, 1).then_inc(s["consts"], 1)
            pool.memset(padding[:, 0:ROW - 1], 0.0).then_inc(s["padding_ready"], 1)
            count(padding[:, ROW - 1:ROW], [[0, 1]], TOKENS, 1).then_inc(s["padding_ready"], 1)
            pool.memset(no_sums[:, :], 0.0).then_inc(s["padding_ready"], 1)
            pool.memset(xn2T, 0.0).then_inc(s["xn2T_kept"], 1)
            pool.wait_ge(s["bias_in"], 16)

            def residual(b):
                pool.wait_ge(s["xn_ready"], b + 1)
                pool.tensor_tensor(x[:, ds(TPB * b, TPB), :], x[:, ds(TPB * b, TPB), :],
                                   spread(bo[:, :], 1, TPB), ALU.add).then_inc(s["res_ready"], 1)

            def keep(b):
                pool.wait_ge(s["xn2T_ready"], b + 1)
                pool.tensor_copy(xn2T_all[:, ds(b, 1), :, :].rearrange("p a k n -> p (a k) n"), xn2T).then_inc(s["xn2T_kept"], 1)

            def scatter(b, par):
                nth = b + 1
                pool.wait_ge(s["slots_ready"], nth)
                pool.tensor_copy(cw[:, ds(TPB * b, TPB), 0:EXPERTS], xn2[:, par, :, D:D + EXPERTS]).then_inc(s["cw_kept"], 1)
                pool.tensor_copy(xn2[:, par, :, ROW - 1:ROW].rearrange("p t a -> p (t a)"), token[:, ds(TPB * b, TPB)]).then_inc(s["copy_ready"], 1)
                wait_apart(pool, s["copy_ready"], nth)
                for j in range(TPB):
                    for k in range(TOPK):
                        pool.indirect_dma_start(
                            dispatch, bass.IndirectOffsetOnAxis(ap=slot_now[:, par, j * TOPK + k:j * TOPK + k + 1], axis=0),
                            xn2[:, par, j, :], None).then_inc(scattered, 16)
                pool.wait_ge(scattered, 16 * TPB * TOPK * (b + 1))

            def step(b, par, front, tail, tail2):
                if tail2:
                    scatter(b - 2, par)
                if front:
                    residual(b + 2)
                if tail:
                    keep(b - 1)

            residual(0)
            residual(1)
            step(0, 0, True, False, False)
            step(1, 1, True, True, False)
            with pool.Fori(MID[0] // 2, MID[1] // 2) as i:
                for u in range(2):
                    step(2 * i + u, u, True, True, True)
            step(BATCHES - 2, 0, False, True, True)
            step(BATCHES - 1, 1, False, True, True)
            scatter(BATCHES - 2, 0)
            keep(BATCHES - 1)
            scatter(BATCHES - 1, 1)

            pool.wait_ge(s["x2_stored"], 16 * BATCHES)
            pool.wait_ge(s["sums_cleared"], 32)

            def combine(i, u):
                first = isinstance(i, int)
                before = added[(u - 2) % UNROLL] if u < 2 or not first else first_added[u - 2]
                used = 16 * i if not first else 16 if u >= 2 else 0
                nth = i + 1
                if not first and u == 0:
                    pool.wait_ge(before, used)
                pool.wait_ge(ey_ready[u], nth)
                pool.tensor_tensor(e_token[:, u:u + 1], e_number[:, u:u + 1], zero1[:, :], ALU.add).then_inc(token_ready[u], 1)
                wait_apart(pool, token_ready[u], nth)
                if u >= 2 or not first and u == 1:
                    pool.wait_ge(before, used)
                done = first_added[u] if first and u < UNROLL - 2 else added[u]
                pool.indirect_dma_start(sums[u % 2], bass.IndirectOffsetOnAxis(ap=e_token[:, u:u + 1], axis=0), e_y[:, u, :], None,
                                        compute_op=ALU.add).then_inc(done, 16)

            for u in range(UNROLL):
                combine(0, u)
            with pool.Fori(1, SLOT_TILES // UNROLL) as i:
                for u in range(UNROLL):
                    combine(i, u)
            for r in range(UNROLL):
                pool.wait_ge(added[r], 16 * (LAST if r < UNROLL - 2 else LAST + 1))
            for r in range(UNROLL - 2):
                pool.wait_ge(first_added[r], 16)
            HALF = TOKENS // 2
            for n in range(2):
                pool.dma_start(out[n * HALF:(n + 1) * HALF, :], odd_sums[n * HALF:(n + 1) * HALF, :], accum_op=ALU.add,
                               max_dma_last_dim=4 * D).then_inc(s["out_done"], 16)
            pool.wait_ge(s["out_done"], 32)

        @block.scalar
        def _(act):
            def norm(b):
                if not isinstance(b, int) or b >= 1:
                    act.wait_ge(s["xnT_psum"], b)
                for j in range(TPB):
                    ins = act.activation(xn[:, j, :], x[:, ds(TPB * b + j, 1), :].rearrange("p a d -> p (a d)"), ACT.Identity,
                                         scale=rstd1[:, ds(TPB * b + j, 1)], bias=nmr1[:, ds(TPB * b + j, 1)])
                ins.then_inc(s["xn_ready"], 1)

            def norm_out(b):
                act.wait_ge(s["xnT_psum"], b + 1)
                act.activation(xnT, psF[:, 2, :].rearrange("p (k n) -> p k n", k=KD), ACT.Copy).then_inc(s["xnT_ready"], 1)

            def q_out(b):
                act.wait_ge(s["q_psum"], b + 1)
                act.activation(qT, psF[:, 2, :].rearrange("p (k n) -> p k n", k=KD), ACT.Copy,
                               scale=float(HD) ** -0.5).then_inc(s["q_ready"], 1)

            def k_out(b):
                act.wait_ge(s["k_psum"], b + 1)
                act.activation(kT, psF[:, 1, :].rearrange("p (k n) -> p k n", k=KD), ACT.Copy).then_inc(s["k_ready"], 1)

            def v_out(b, par):
                act.wait_ge(s["v_psum"], b + 1)
                act.activation(v_sb[:, par], psF[:, 0, :].rearrange("p (k n) -> p k n", k=2), ACT.Copy).then_inc(s["v_ready"], 1)

            def exps(b):
                for j in range(TPB):
                    act.wait_ge(s["nmax_ready"], TPB * b + (j + 1))
                    for hp in range(HEADS):
                        ins = act.activation(probs[:, j, hp, :], psS[:, 2 * j + hp // 2, (hp % 2) * LQ:(hp % 2 + 1) * LQ], ACT.Exp,
                                             bias=nmax[:, j, hp:hp + 1], accum_out=psums[:, j, hp:hp + 1])
                    ins.then_inc(s["probs_ready"], 1)

            def gate_exps(b):
                act.wait_ge(s["gate_shifted"], b + 1)
                act.activation(gexp[:, :, :], logit[:, :, :], ACT.Exp).then_inc(s["gate_exp"], 1)

            def probs_out(b):
                for j in range(TPB):
                    act.wait_ge(s["pT_psum"], TPB * b + (j + 1))
                    act.activation(pT[:, j], psS[:, 2 * j:2 * j + 2, :].rearrange("p t (h q) -> p t h q", h=HEADS), ACT.Copy).then_inc(s["pT_ready"], 1)

            def attend_out(b):
                act.wait_ge(s["attT_psum"], b + 1)
                act.activation(attT, psF[:, 0, :].rearrange("p (t k q) -> p t k q", t=TPB, k=KD), ACT.Copy).then_inc(s["attT_ready"], 1)

            def step(b, par, front, front2, tail):
                if front:
                    q_out(b + 1)
                    k_out(b + 1)
                    v_out(b + 1, 1 - par)
                else:
                    silu(0, 0)
                if tail:
                    norm2_out(b - 1)
                probs_out(b)
                if tail:
                    gate_exps(b - 1)
                if front2:
                    norm(b + 2)
                attend_out(b)
                if front2:
                    norm_out(b + 2)
                if front:
                    exps(b + 1)

            def norm2_out(b):
                act.wait_ge(s["xn2T_psum"], b + 1)
                act.wait_ge(s["xn2T_kept"], b + 1)
                act.activation(xn2T, psG[:, :].rearrange("p (k n) -> p k n", k=KD), ACT.Copy).then_inc(s["xn2T_ready"], 1)

            def weights_now(c):
                act.wait_ge(s["cw_kept"], c + 1)
                if c >= 1:
                    act.wait_ge(s["cwT_psum"], c)
                act.activation(cw_now[:, :, :], cw[:, TPB * c:TPB * c + TPB, :], ACT.Copy).then_inc(s["cw_copied"], 1)

            def weights_out(c):
                act.wait_ge(s["cwT_psum"], c + 1)
                if c >= 1:
                    act.wait_ge(s["sh_out_psum"], c)
                act.activation(cwT[:, :, :], psF[0:EXPERTS + 1, 2, 0:LQ].rearrange("p (t q) -> p t q", t=TPB), ACT.Copy).then_inc(s["cwT_ready"], 1)

            def silu(c, par):
                for m in range(KS):
                    act.wait_ge(s["sh_psum"], KS * c + (m + 1))
                    act.activation(hs[:, par, m, :], shared_bank(c, m)[:, 0:LQ], ACT.Silu, bias=sb13[:, m:m + 1]).then_inc(s["sh_silu"], 1)

            act.wait_ge(s["norm1"], 1)
            norm(0)
            k_out(0)
            norm_out(0)
            v_out(0, 0)
            q_out(0)
            act.wait_ge(s["norm1"], 2)
            norm(1)
            norm_out(1)
            exps(0)
            act.wait_ge(s["norm1"], 3)
            step(0, 0, True, True, False)
            step(1, 1, True, True, True)
            with act.Fori(MID[0] // 2, MID[1] // 2) as i:
                for u in range(2):
                    step(2 * i + u, u, True, True, True)
            step(BATCHES - 2, 0, True, False, True)
            step(BATCHES - 1, 1, False, False, True)

            last = BATCHES - 1
            weights_now(0)
            silu(1, 1)
            weights_out(0)
            norm2_out(last)
            for c in range(1, BATCHES):
                weights_now(c)
                if c + 1 < BATCHES:
                    silu(c + 1, (c + 1) % 2)
                weights_out(c)
                if c == 1:
                    gate_exps(last)
                if c == 3:
                    act.wait_ge(s["table_psum"], 1)
                    act.activation(table[0:1, :, :], psG[0:1, 0:2 * P].rearrange("p (a t) -> p a t", a=2), ACT.Copy).then_inc(s["table_ready"], 1)

            def experts(i, u):
                if lies(i, u, -2):
                    t, _, _ = ring(i, u, -2)
                    act.wait_ge(s["emT_psum"], t + 1)
                    act.activation(e_mT[:, u % 2, :], psF[:, u % 2, 0:P], ACT.Copy).then_inc(s["emT_ready"], 1)
                if lies(i, u, 2):
                    t, _, _ = ring(i, u, 2)
                    act.wait_ge(s["exT_psum"], t + 1)
                    act.activation(e_xT[:, (u + 2) % 3], psS[:, u % 2, 0:D].rearrange("p (k q) -> p k q", k=KD), ACT.Copy).then_inc(s["exT_ready"], 1)
                if lies(i, u, 0):
                    t, r, n = ring(i, u, 0)
                    if not isinstance(n, int) or n >= 1:
                        act.wait_ge(token_ready[r], n)
                    act.activation(e_meta[:, r, :], e_x[:, r, D:ROW - 1], ACT.Copy)
                    act.activation(e_number[:, r:r + 1], e_x[:, r, ROW - 1:ROW], ACT.Copy).then_inc(s["meta_copied"], 1)
                if lies(i, u, 0):
                    t, _, _ = ring(i, u, 0)
                    act.wait_ge(s["eh_ready"], t + 1)
                    act.activation(e_g[:, u % 2, :], e_h[:, u % 2, 0:INTER], ACT.Silu).then_inc(s["eg_ready"], 1)

            run_slots(act, experts)

        @block.tensor
        def _(pe):

            def norm_T(b):
                pe.wait_ge(s["xn_ready"], b + 1)
                for j in range(TPB):
                    for k in range(KD):
                        ins = pe.transpose(psF[:, 2, k * LQ + j * P:k * LQ + (j + 1) * P], xn[:, j, k * P:(k + 1) * P], ident[:, :])
                ins.then_inc(s["xnT_psum"], 1)

            def proj_q(b):
                pe.wait_ge(s["xnT_ready"], b + 1)
                for m in range(KD):
                    for k in range(KD):
                        ins = pe.matmul(psF[:, 2, m * LQ:(m + 1) * LQ], wq[:, k, m * P:(m + 1) * P], xnT[:, k, :],
                                        start=(k == 0), stop=(k == KD - 1))
                ins.then_inc(s["q_psum"], 1)

            def proj_k(b, par, nth):
                pe.wait_ge(ctx_in[par], 16 * nth)
                if not isinstance(b, int) or b >= 2:
                    pe.wait_ge(s["x1_ready"], b - 1)
                for m in range(KD):
                    for k in range(2):
                        ins = pe.matmul(psF[:, 1, m * LQ:(m + 1) * LQ], wk[0:KC, k, m * P:(m + 1) * P],
                                        ctx_now[0:KC, par, k, :], start=(k == 0), stop=(k == 1))
                ins.then_inc(s["k_psum"], 1)

            def proj_v(b, par):
                for t in range(2):
                    for k in range(2):
                        ins = pe.matmul(psF[:, 0, t * D:(t + 1) * D], ctx_now[0:KC, par, k, t * P:(t + 1) * P], wv[0:KC, k, :],
                                        start=(k == 0), stop=(k == 1))
                ins.then_inc(s["v_psum"], 1)

            def scores(b, j):
                if j == 0:
                    pe.wait_ge(s["q_ready"], b + 1)
                    pe.wait_ge(s["k_ready"], b + 1)
                for h in range(HEADS):
                    r = HD * (h % 2)
                    ins = pe.matmul(psS[:, 2 * j + h % 2, (h // 2) * LQ:(h // 2 + 1) * LQ], qT[r:r + HD, h // 2, j * P:(j + 1) * P],
                                    kT[r:r + HD, h // 2, :], start=True, stop=True)
                ins.then_inc(s["scores_psum"], 1)

            def probs_T(b, j):
                pe.wait_ge(s["probs_ready"], TPB * b + (j + 1))
                for t in range(2):
                    for hp in range(HEADS):
                        ins = pe.transpose(psS[:, 2 * j + t, hp * P:(hp + 1) * P], probs[:, j, hp, t * P:(t + 1) * P], ident[:, :])
                ins.then_inc(s["pT_psum"], 1)

            def attend(b, j, par, front):
                pe.wait_ge(s["pT_ready"], TPB * b + (j + 1))
                pe.wait_ge(s["v_ready"], b + 1)
                if front:
                    pe.wait_ge(s["q_ready" if j == 0 else "k_ready"], b + 2)
                elif j == 1:
                    pe.wait_ge(s["sh_ready"], KS)
                for hp in range(HEADS):
                    h = (hp % 2) * 2 + hp // 2
                    for t in range(2):
                        ins = pe.matmul(psF[:, 2 - j, h * HD:(h + 1) * HD], pT[:, j, t, hp, :], v_sb[:, par, t, h * HD:(h + 1) * HD],
                                        start=(t == 0), stop=(t == 1))
                ins.then_inc(s["att_psum"], 1)

            def attend_T(b, front):
                for j in range(TPB):
                    pe.wait_ge(s["att_ready"], TPB * b + (j + 1))
                    if front and j == 0:
                        pe.wait_ge(s["v_ready"], b + 2)
                    for k in range(KD):
                        ins = pe.transpose(psF[:, 0, j * LQ + k * P:j * LQ + (k + 1) * P], att[:, j, k * P:(k + 1) * P], ident[:, :])
                ins.then_inc(s["attT_psum"], 1)

            def project(b):
                pe.wait_ge(s["attT_ready"], b + 1)
                for j in range(TPB):
                    for k in range(KD):
                        ins = pe.matmul(psF[:, 1, j * D:(j + 1) * D], attT[:, j, k, :], wo[:, k, :], start=(k == 0), stop=(k == KD - 1))
                ins.then_inc(s["proj_psum"], 1)

            def norm2_T(b, par):
                pe.wait_ge(s["xn2_ready"], b + 1)
                if not isinstance(b, int) or b >= 1:
                    pe.wait_ge(s["rank_taken"], b + 1)
                for j in range(TPB):
                    for k in range(KD):
                        ins = pe.transpose(psG[:, k * LQ + j * P:k * LQ + (j + 1) * P], xn2[:, par, j, k * P:(k + 1) * P], ident[:, :])
                ins.then_inc(s["xn2T_psum"], 1)

            def gate(b):
                pe.wait_ge(s["xn2T_ready"], b + 1)
                for j in range(TPB):
                    for k in range(KD):
                        ins = pe.matmul(psG[:, j * EXPERTS:(j + 1) * EXPERTS], xn2T[:, k, j * P:(j + 1) * P], gw[:, k, :],
                                        start=(k == 0), stop=(k == KD - 1))
                ins.then_inc(s["gate_psum"], 1)

            def ranks(b):
                pe.wait_ge(s["chosen_ready"], b + 1)
                pe.matmul(psG[:, 0:32], earlier[:, :], chosen[:, 0, :], start=True, stop=True)
                pe.matmul(psG[:, 32:64], earlier[:, :], chosen[:, 1, :], start=True, stop=False)
                pe.matmul(psG[:, 32:64], ones[:, :], chosen[:, 0, :], start=False, stop=True)
                pe.matmul(psG[:, 64:96], ones[:, :], chosen[:, 0, :], start=True, stop=False)
                pe.matmul(psG[:, 64:96], ones[:, :], chosen[:, 1, :], start=False, stop=True).then_inc(s["rank_psum"], 1)

            def shared_up(c, par):
                pe.wait_ge(s["xn2T_kept"], c + 2)
                if c >= 2:
                    pe.wait_ge(s["sh_ready"], KS * (c - 1))
                for m in range(KS):
                    for n in range(2):
                        for k in range(KD):
                            ins = pe.matmul(shared_bank(c, m)[:, n * LQ:(n + 1) * LQ], sw13[:, k, n * SHARED + m * P:n * SHARED + (m + 1) * P],
                                            xn2T_all[:, c, k, :], start=(k == 0), stop=(k == KD - 1))
                    ins.then_inc(s["sh_psum"], 1)

            def shared_down(c, par):
                pe.wait_ge(s["cw_copied"], c + 1)
                if c >= 1:
                    pe.wait_ge(s["cwT_ready"], c)
                for j in range(TPB):
                    ins = pe.transpose(psF[0:EXPERTS + 1, 2, j * P:(j + 1) * P], cw_now[:, j, :], ident[:, :])
                ins.then_inc(s["cwT_psum"], 1)
                pe.wait_ge(s["sh_ready"], KS * c + KS)
                if c >= 2:
                    pe.wait_ge(s["sh_added"], c - 1)
                else:
                    pe.wait_ge(s["x1_ready"], BATCHES)
                for j in range(TPB):
                    y = psF[:, c % 2, j * D:(j + 1) * D]
                    for m in range(KS):
                        pe.matmul(y, hs[:, par, m, j * P:(j + 1) * P], sw2[:, m, :], start=(m == 0), stop=False)
                    if j == 0:
                        pe.wait_ge(s["cwT_ready"], c + 1)
                    ins = pe.matmul(y, cwT[:, j, :], b2[:, :], start=False, stop=True)
                ins.then_inc(s["sh_out_psum"], 1)

            def step(b, par, front, front2, tail, tail2, nth):
                if front:
                    proj_q(b + 1)
                    proj_k(b + 1, 1 - par, nth)
                else:
                    pe.wait_ge(s["x1_ready"], b)
                    shared_up(0, 0)
                if tail2:
                    ranks(b - 2)
                if front:
                    proj_v(b + 1, 1 - par)
                if tail:
                    norm2_T(b - 1, 1 - par)
                for j in range(TPB):
                    probs_T(b, j)
                if tail:
                    gate(b - 1)
                for j in range(TPB):
                    attend(b, j, par, front)
                if front:
                    scores(b + 1, 0)
                attend_T(b, front)
                if front2:
                    norm_T(b + 2)
                if front:
                    scores(b + 1, 1)
                project(b)

            pe.wait_ge(s["wk_in"], 16)
            proj_k(0, 0, 1)
            pe.wait_ge(s["consts"], CONSTS - 4)
            norm_T(0)
            pe.wait_ge(s["wv_in"], 16)
            proj_v(0, 0)
            pe.wait_ge(s["wq_in"], 16)
            proj_q(0)
            scores(0, 0)
            norm_T(1)
            scores(0, 1)
            pe.wait_ge(s["wo_in"], 16)
            pe.wait_ge(s["gate_in"], 32)
            step(0, 0, True, True, False, False, 1)
            step(1, 1, True, True, True, False, 2)
            with pe.Fori(MID[0] // 2, MID[1] // 2) as i:
                for u in range(2):
                    step(2 * i + u, u, True, True, True, True, i + (u + 1))
            step(BATCHES - 2, 0, True, False, True, True, BATCHES // 2)
            pe.wait_ge(s["shared_in"], 64)
            step(BATCHES - 1, 1, False, False, True, True, None)

            last = BATCHES - 1
            shared_up(1, 1)
            ranks(last - 1)
            shared_down(0, 0)
            norm2_T(last, 1)
            for c in range(1, BATCHES):
                if c + 1 < BATCHES:
                    shared_up(c + 1, (c + 1) % 2)
                if c == 1:
                    gate(last)
                shared_down(c, c % 2)
                if c == 2:
                    ranks(last)
                if c == 3:
                    pe.wait_ge(s["table_cols"], 2)
                    for n in range(2):
                        ins = pe.matmul(psG[0:1, n * P:(n + 1) * P], cols[:, n:n + 1], ident[:, :], start=True, stop=True)
                    ins.then_inc(s["table_psum"], 1)

            tile_experts = TileExperts(pe, table)

            def experts(i, u):
                if lies(i, u, 0):
                    pe.wait_ge(s["exT_ready"], ring(i, u, 0)[0] + 1)
                if lies(i, u, 2):
                    t, r, n = ring(i, u, 2)
                    pe.wait_ge(rows_in[r], 16 * (n + 1))
                    for k in range(KD):
                        ins = pe.transpose(psS[:, u % 2, k * P:(k + 1) * P], e_x[:, r, k * P:(k + 1) * P], ident[:, :])
                    ins.then_inc(s["exT_psum"], 1)
                if lies(i, u, -2):
                    t, _, _ = ring(i, u, -2)
                    pe.wait_ge(s["em_ready"], t + 1)
                    pe.transpose(psF[:, u % 2, 0:P], e_m[:, u % 2, :], ident[:, :]).then_inc(s["emT_psum"], 1)
                if lies(i, u, -3):
                    t, _, _ = ring(i, u, -3)
                    pe.wait_ge(s["emT_ready"], t + 1)
                    if lies(i, u, -5):
                        _, r, n = ring(i, u, -5)
                        pe.wait_ge(ey_ready[r], n + 1)
                    pe.matmul(psF[:, 2, 0:D] if u % 2 else psG[:, 0:D], e_mT[:, (u + 1) % 2, :],
                              w2[:, ds(tile_experts.of(u, -3), 1), :].rearrange("p a n -> p (a n)"), start=True, stop=True).then_inc(s["ey_psum"], 1)
                if lies(i, u, 0):
                    t, _, _ = ring(i, u, 0)
                    if lies(i, u, -2):
                        pe.wait_ge(s["eh_ready"], t - 1)
                    for k in range(KD):
                        ins = pe.matmul(psS[:, 2 + u % 2, 0:2 * INTER], e_xT[:, u % 3, k, :],
                                        w13[:, ds(tile_experts.of(u, 0), 1), k, :].rearrange("p a n -> p (a n)"), start=(k == 0), stop=(k == KD - 1))
                    ins.then_inc(s["eh_psum"], 1)

            pe.wait_ge(s["w_in"], 16 * 2 * BATCHES)
            pe.wait_ge(s["table_ready"], 1)
            pe.wait_ge(s["sh_ready"], KS * BATCHES)
            pe.wait_ge(s["sh_added"], BATCHES)
            run_slots(pe, experts, tile_experts.begin)

        @block.vector
        def _(dve):
            st = Steps(dve, s["v_steps"])

            def rsqrt_guess(n, var):
                w, y = rsq[:, 0, 0:n], rsq[:, 1, 0:n]
                st.did(dve.tensor_scalar(w, var, EPS, None, ALU.add), "var")
                st.need("var")
                st.did(dve.tensor_scalar(y.bitcast(I32), w.bitcast(I32), 1, None, ALU.arith_shift_right), "half")
                st.need("half")
                st.did(dve.tensor_scalar(y.bitcast(I32), y.bitcast(I32), -1.0, float(RSQRT_MAGIC), ALU.mult, ALU.add), "root")

            def rsqrt_refine(n, tmp, to=None):
                w, y = rsq[:, 0, 0:n], rsq[:, 1, 0:n]
                st.need("root")
                st.did(dve.tensor_tensor(tmp, w, y, ALU.mult), "wy")
                st.need("wy")
                st.did(dve.scalar_tensor_tensor(tmp, tmp, -0.5, y, ALU.mult, ALU.mult), "wyy")
                st.need("wyy")
                st.did(dve.scalar_tensor_tensor(y if to is None else to, tmp, 1.5, y, ALU.add, ALU.mult), "root")

            for loaded, t0, t1 in (("x0_in", 0, TPB), ("x1_in", TPB, 2 * TPB), ("xr_in", 2 * TPB, TILES)):
                dve.wait_ge(s[loaded], 16)
                for t in range(t0, t1):
                    st.did(dve.bn_stats(st1[:, t, :], x[:, t, :]), f"stats{t}")
                for t in range(t0, t1):
                    st.need(f"stats{t}")
                    st.did(dve.bn_aggr(mv1[:, t, :], st1[:, t, :]), f"aggr{t}")
                st.need(f"aggr{t1 - 1}")
                rsqrt_guess(t1 - t0, mv1[:, t0:t1, 1])
                for r in range(3):
                    rsqrt_refine(t1 - t0, rstd1[:, t0:t1], rstd1[:, t0:t1] if r == 2 else None)
                st.need("root")
                dve.scalar_tensor_tensor(nmr1[:, t0:t1], mv1[:, t0:t1, 0], -1.0, rstd1[:, t0:t1], ALU.mult, ALU.mult).then_inc(s["norm1"], 1)
            dve.wait_ge(s["consts"], CONSTS - 4)
            dve.wait_ge(s["gate_in"], 32)
            dve.tensor_copy(base[:, :], region0[:, :]).then_inc(s["rank_taken"], 1)

            def maxima(b, j):
                dve.wait_ge(s["scores_psum"], TPB * b + (j + 1))
                dve.tensor_reduce(nmax[:, j, :], psS[:, 2 * j:2 * j + 2, :].rearrange("p a (c n) -> p a c n", c=2), X, ALU.max,
                                  negate=True).then_inc(s["nmax_ready"], 1)

            def gate_shift(b):
                dve.wait_ge(s["gate_psum"], b + 1)
                st.did(dve.tensor_tensor(logit[:, :, :], psG[:, 0:TPB * EXPERTS].rearrange("p (t e) -> p t e", t=TPB),
                                         spread(gb[:, :], 1, TPB), ALU.add), "logit")
                st.need("logit")
                st.did(dve.tensor_reduce(gmax[:, :], logit[:, :, :], X, ALU.max), "gmax")
                st.need("gmax")
                dve.tensor_tensor(logit[:, :, :], logit[:, :, :], spread(gmax[:, :], 2, EXPERTS), ALU.subtract).then_inc(s["gate_shifted"], 1)

            def route_groups(b):
                dve.wait_ge(s["gate_exp"], b + 1)
                st.did(dve.tensor_reduce(gsum[:, :], gexp[:, :, :], X, ALU.add), "gsum")
                st.need("gsum")
                st.did(dve.reciprocal(gsum[:, :], gsum[:, :]), "grcp")
                st.need("grcp")
                st.did(dve.tensor_tensor(score[:, :, :], gexp[:, :, :], spread(gsum[:, :], 2, EXPERTS), ALU.mult), "score")
                st.need("score")
                sv = score[:, :, :].rearrange("p t (g c) -> p (t g) c", c=GSIZE)
                st.did(dve.tensor_tensor(hi2[:, :, :], sv[:, :, 0:2], sv[:, :, 2:4], ALU.max), "hi2")
                st.did(dve.tensor_tensor(lo2[:, :, :], sv[:, :, 0:2], sv[:, :, 2:4], ALU.min), "lo2")
                st.need("hi2")
                st.did(dve.tensor_tensor(first[:, :], hi2[:, :, 0], hi2[:, :, 1], ALU.max), "first")
                st.did(dve.tensor_tensor(secnd[:, :], hi2[:, :, 0], hi2[:, :, 1], ALU.min), "secnd")
                st.need("lo2")
                st.did(dve.tensor_tensor(third[:, :], lo2[:, :, 0], lo2[:, :, 1], ALU.max), "third")
                st.need("third")
                st.did(dve.tensor_tensor(secnd[:, :], secnd[:, :], third[:, :], ALU.max), "second")
                st.need("second")
                st.did(dve.tensor_tensor(gscore[:, :, :].rearrange("p t g -> p (t g)"), first[:, :], secnd[:, :], ALU.add), "gscore")
                st.need("gscore")
                other, own = spread(gscore[:, :, :], 2, GROUPS), spread(gscore[:, :, :], 3, GROUPS)
                st.did(dve.tensor_tensor(ties[:, :, :, :], other, own, ALU.is_equal), "equal")
                st.did(dve.tensor_tensor(beats[:, :, :, :], other, own, ALU.is_gt), "beats")
                st.need("equal")
                st.did(dve.tensor_tensor(ties[:, :, :, :].rearrange("p t g h -> p t (g h)"), ties[:, :, :, :].rearrange("p t g h -> p t (g h)"),
                                         spread(lower[:, :, :].rearrange("p g h -> p (g h)"), 1, TPB), ALU.mult), "ties")
                st.need("ties")
                st.did(dve.tensor_tensor(beats[:, :, :, :], beats[:, :, :, :], ties[:, :, :, :], ALU.add), "ahead")
                st.need("ahead")
                st.did(dve.tensor_reduce(grank[:, :, :], beats[:, :, :, :], X, ALU.add), "grank")
                st.need("grank")
                st.did(dve.tensor_scalar(keep[:, :, :], grank[:, :, :], TOPG - 0.5, None, ALU.is_lt), "keep")
                st.did(dve.tensor_scalar(keep1[:, :, :], grank[:, :, :], TOPG - 0.5, 1.0, ALU.is_lt, ALU.subtract), "keep1")

            def route_experts(b, par):
                sv = score[:, :, :].rearrange("p t (g c) -> p (t g) c", c=GSIZE)
                mv = masked[:, :, :].rearrange("p t (g c) -> p (t g) c", c=GSIZE)
                kv, k1 = (z[:, :, :].rearrange("p t g -> p (t g)") for z in (keep, keep1))
                st.need("keep1")
                st.did(dve.tensor_tensor(mv, sv, spread(kv, 2, GSIZE), ALU.mult), "kept")
                st.need("kept")
                dve.tensor_tensor(mv, mv, spread(k1, 2, GSIZE), ALU.add).then_inc(s["masked_ready"], 1)
                wait_apart(dve, s["masked_ready"], b + 1)
                for j in range(TPB):
                    dve.max(top[:, j, :], masked[:, j, :]).then_inc(top_ready[j], 1)
                for j in range(TPB):
                    wait_apart(dve, top_ready[j], b + 1)
                    st.did(dve.max_index(topi[:, j, :], top[:, j, :], masked[:, j, :]), f"topi{j}")
                st.need(f"topi{TPB - 1}")
                st.did(dve.tensor_copy(topf[:, :, :], topi[:, :, 0:TOPK]), "topf")
                st.need("topf")
                st.did(dve.tensor_tensor(onehot[:, :, :, :].rearrange("p t k e -> p (t k) e"), spread(iota_e[:, :], 1, TPB * TOPK),
                                         spread(topf[:, :, :].rearrange("p t k -> p (t k)"), 2, EXPERTS), ALU.is_equal), "onehot")
                st.need("onehot")
                with nc.allow_low_precision("zeros and ones"):
                    ins = dve.tensor_reduce(chosen[:, :, :], onehot[:, :, :, :].rearrange("p t k e -> p t e k"), X, ALU.add)
                st.did(ins, "chosen")
                st.need("chosen")
                dve.tensor_tensor(xn2[:, par, :, D:D + EXPERTS], score[:, :, :], chosen[:, :, :], ALU.mult).then_inc(s["chosen_ready"], 1)

            def rank_take(b):
                dve.wait_ge(s["rank_psum"], b + 1)
                dve.wait_ge(s["rank_taken"], b + 1)
                st.did(dve.tensor_tensor(rowof[:, :, :], psG[:, 0:TPB * EXPERTS].rearrange("p (t e) -> p t e", t=TPB),
                                         spread(base[:, :], 1, TPB), ALU.add), "rowof")
                st.need("rowof")
                dve.tensor_tensor(base[:, :], psG[:, 64:64 + EXPERTS], base[:, :], ALU.add).then_inc(s["rank_taken"], 1)

            def rank_pick(j):
                st.need("rowof")
                st.did(dve.tensor_tensor(picked[:, j], onehot[:, j], spread(rowof[:, j, :], 1, TOPK), ALU.mult), f"picked{j}")

            def rank_sum():
                st.need(f"picked{TPB - 1}")
                st.did(dve.tensor_reduce(row_now[:, :, :], picked[:, :, :, :], X, ALU.add), "rows")

            def rank_out(par):
                st.need("rows")
                dve.tensor_copy(slot_now[:, par, :], row_now[:, :, :].rearrange("p t k -> p (t k)")).then_inc(s["slots_ready"], 1)

            def attend_out(b):
                dve.wait_ge(s["probs_ready"], TPB * b + 2)
                st.did(dve.reciprocal(prcp[:, :, :], psums[:, :, :]), "prcp")
                st.need("prcp")
                for j in range(TPB):
                    dve.wait_ge(s["att_psum"], TPB * b + (j + 1))
                    dve.tensor_tensor(att[:, j, :].rearrange("p (h l d) -> p l h d", l=2, d=HD),
                                      psF[:, 2 - j, 0:D].rearrange("p (h l d) -> p l h d", l=2, d=HD),
                                      spread(prcp[:, j, :].rearrange("p (l h) -> p l h", l=2), 3, HD), ALU.mult).then_inc(s["att_ready"], 1)

            def rows_of(b, j):
                return x[:, ds(TPB * b + j, 1), :].rearrange("p a d -> p (a d)")

            def residual(b):
                dve.wait_ge(s["res_ready"], b + 1)
                dve.wait_ge(s["proj_psum"], b + 1)
                xt = x[:, ds(TPB * b, TPB), :]
                dve.tensor_tensor(xt, psF[:, 1, :].rearrange("p (t d) -> p t d", t=TPB), xt, ALU.add).then_inc(s["x1_ready"], 1)

            def norm2(b, par, tail):
                for j in range(TPB):
                    wait_apart(dve, s["x1_ready"], b + 1)
                    dve.bn_stats(st2[:, j, :], rows_of(b, j)).then_inc(stats_ready[j], 1)
                for j in range(TPB):
                    wait_apart(dve, stats_ready[j], b + 1)
                    ins = dve.bn_aggr(mv2[:, j, :], st2[:, j, :])
                st.did(ins, "aggr")
                st.need("aggr")
                rsqrt_guess(TPB, mv2[:, :, 1])
                rsqrt_refine(TPB, rstd2[:, :])
                rsqrt_refine(TPB, rstd2[:, :])
                if tail:
                    rank_take(b - 1)
                rsqrt_refine(TPB, rstd2[:, :], rstd2[:, :])
                if tail:
                    rank_pick(0)
                    rank_pick(1)
                st.need("root")
                if not isinstance(b, int) or b >= 2:
                    dve.wait_ge(s["xn2T_kept"], b + 1)
                for j in range(TPB):
                    ins = dve.tensor_scalar(xn2[:, par, j, 0:D], rows_of(b, j), mv2[:, j, 0:1], rstd2[:, j:j + 1], ALU.subtract, ALU.mult)
                ins.then_inc(s["xn2_ready"], 1)
                if tail:
                    rank_sum()
                    rank_out(1 - par)

            def shared_hidden(c, par):
                for m in range(KS):
                    dve.wait_ge(s["sh_silu"], KS * c + (m + 1))
                    dve.scalar_tensor_tensor(hs[:, par, m, :], shared_bank(c, m)[:, LQ:2 * LQ], sb13[:, KS + m:KS + m + 1], hs[:, par, m, :],
                                             ALU.add, ALU.mult).then_inc(s["sh_ready"], 1)

            def shared_add(c):
                dve.wait_ge(s["sh_out_psum"], c + 1)
                xt = x[:, TPB * c:TPB * c + TPB, :]
                dve.tensor_tensor(xt, psF[:, c % 2, :].rearrange("p (t d) -> p t d", t=TPB), xt, ALU.add).then_inc(s["sh_added"], 1)

            def step(b, par, front, tail, tail2):
                if tail:
                    residual(b - 1)
                    norm2(b - 1, 1 - par, tail2)
                    if not front:
                        shared_hidden(0, 0)
                    gate_shift(b - 1)
                    route_groups(b - 1)
                attend_out(b)
                if front:
                    maxima(b + 1, 0)
                if tail:
                    route_experts(b - 1, 1 - par)
                if front:
                    maxima(b + 1, 1)

            maxima(0, 0)
            maxima(0, 1)
            step(0, 0, True, False, False)
            step(1, 1, True, True, False)
            start = st.n
            with dve.Fori(0, (MID[1] - MID[0]) // 2) as i:
                for u in range(2):
                    st.body(start + (i * (2 * STEP_COUNT) + u * STEP_COUNT))
                    step(2 * i + (MID[0] + u), u, True, True, True)
                    assert st.n == STEP_COUNT, st.n
            st.body(start + (MID[1] - MID[0]) * STEP_COUNT)
            step(BATCHES - 2, 0, True, True, True)
            step(BATCHES - 1, 1, False, True, True)

            last = BATCHES - 1
            residual(last)
            norm2(last, 1, True)
            shared_hidden(1, 1)
            shared_add(0)
            gate_shift(last)
            shared_hidden(2, 0)
            route_groups(last)
            route_experts(last, 1)
            shared_add(1)
            shared_hidden(3, 1)
            rank_take(last)
            dve.wait_ge(s["rank_taken"], BATCHES + 1)
            dve.tensor_copy(tail_row[:, :], base[0:1, :]).then_inc(s["tail_rows"], 1)
            rank_pick(0)
            rank_pick(1)
            rank_sum()
            rank_out(1)

            st.did(dve.memset(cnt[:, :, :], 0.0), "cnt0")
            st.did(dve.scalar_tensor_tensor(cnti[:, :], base[:, :], float(P - 1), region0[:, :], ALU.add, ALU.subtract), "tokens")
            st.need("tokens")
            st.did(dve.tensor_scalar(cnti[:, :], cnti[:, :], P.bit_length() - 1, None, ALU.arith_shift_right), "tiles")
            st.need("tiles")
            st.need("cnt0")
            st.did(dve.tensor_copy(cnt[:, 0, PAD:], cnti[:, :]), "prefix0")
            k, cur, n = 1, 0, 0
            while k < EXPERTS:
                st.need(f"prefix{n}")
                n += 1
                st.did(dve.tensor_tensor(cnt[:, 1 - cur, PAD:], cnt[:, cur, PAD:], cnt[:, cur, PAD - k:PAD + EXPERTS - k], ALU.add), f"prefix{n}")
                k, cur = 2 * k, 1 - cur
            ends, before, start_t = cnt[:, cur, PAD:], cnt[:, 1 - cur, PAD:], cnt[:, 2, 0:1]
            st.need(f"prefix{n}")
            st.did(dve.tensor_scalar(before, ends, iota_p[:, 0:1], None, ALU.is_le), "before")
            st.need("before")
            st.did(dve.tensor_reduce(cols[:, 2:3], before, X, ALU.add), "expert")
            st.did(dve.tensor_tensor(before, before, ends, ALU.mult), "ended")
            st.need("ended")
            st.did(dve.tensor_reduce(start_t, before, X, ALU.max), "start")
            st.need("start")
            st.did(dve.tensor_tensor(start_t, iota_p[:, 0:1], start_t, ALU.subtract), "nth")
            st.did(dve.tensor_scalar(cols[:, 3:4], cols[:, 2:3], EXPERTS - 0.5, float(P), ALU.is_lt, ALU.mult), "rows")
            st.need("rows")
            st.did(dve.tensor_tensor(start_t, start_t, cols[:, 3:4], ALU.mult), "into")
            st.need("into")
            dve.tensor_scalar(cols[:, 0:1], cols[:, 2:3], EXPERTS - 1.0, None, ALU.min).then_inc(s["table_cols"], 1)
            dve.scalar_tensor_tensor(cols[:, 1:2], cols[:, 2:3], float(REGION), start_t, ALU.mult, ALU.add).then_inc(s["table_cols"], 1)
            shared_hidden(4, 0)
            shared_add(2)
            for c in range(3, BATCHES):
                shared_add(c)
                if c + 2 < BATCHES:
                    shared_hidden(c + 2, c % 2)

            tile_experts = TileExperts(dve, table)

            def experts(i, u):
                if lies(i, u, -1):
                    t, _, _ = ring(i, u, -1)
                    dve.wait_ge(s["eg_ready"], t + 1)
                    dve.tensor_tensor(e_m[:, (u + 1) % 2, :], e_g[:, (u + 1) % 2, :], e_h[:, (u + 1) % 2, INTER:], ALU.mult).then_inc(s["em_ready"], 1)
                if lies(i, u, -3):
                    t, r, n = ring(i, u, -3)
                    dve.wait_ge(s["ey_psum"], t + 1)
                    if lies(i, u, -9):
                        _, r6, n6 = ring(i, u, -6)
                        dve.wait_ge(token_ready[r6], n6 + 1)
                    dve.tensor_scalar(e_y[:, r, :], psF[:, 2, 0:D] if u % 2 else psG[:, 0:D], e_meta[:, r, ds(tile_experts.of(u, -3), 1)], None,
                                      ALU.mult).then_inc(ey_ready[r], 1)
                if lies(i, u, 0):
                    t, _, _ = ring(i, u, 0)
                    dve.wait_ge(s["eh_psum"], t + 1)
                    dve.tensor_tensor(e_h[:, u % 2, :], psS[:, 2 + u % 2, 0:2 * INTER], b13[:, ds(tile_experts.of(u, 0) * (2 * INTER), 2 * INTER)],
                                      ALU.add).then_inc(s["eh_ready"], 1)

            dve.wait_ge(s["table_ready"], 1)
            dve.wait_ge(s["b13_in"], 16)
            run_slots(dve, experts, tile_experts.begin)


_OUT = (BATCHES, LQ, D)


def _halves(w):
    return w.reshape(2, w.shape[0] // 2, -1).transpose(1, 0, 2)


def kernel(**inputs):
    import numpy as np
    import concourse.bacc as bacc
    from concourse import mybir as mb
    from concourse.bass_utils import run_bass_kernel_spmd

    g = {n: np.asarray(v) for n, v in inputs.items()}
    f = {n[len("L0_ffn_"):]: v for n, v in g.items() if n.startswith("L0_ffn_")}
    t = {n[len("L0_xattn_"):]: v for n, v in g.items() if n.startswith("L0_xattn_")}
    w13 = np.concatenate([f["w1"], f["w3"]], axis=2)
    laid = {
        "x": g["x"].reshape(TOKENS, D),
        "ctxT": _halves(g["ctx_768"].reshape(TOKENS, DKV).T),
        "wq": _halves(t["Wq"].T), "wk": _halves(t["Wk"].T), "wv": _halves(t["Wv"].T), "wo": _halves(t["Wo"].T),
        "bo": t["bo"], "gw": _halves(f["gw"]), "gb": f["gb"],
        "w13": w13.reshape(EXPERTS, KD, P, 2 * INTER).transpose(2, 0, 1, 3),
        "w2": f["w2"].transpose(1, 0, 2),
        "b13": np.concatenate([f["b1"], f["b3"]], axis=1).reshape(-1),
        "b2": np.concatenate([f["b2"], f["sb2"][None]], axis=0),
        "sw13": _halves(np.concatenate([f["sw1"], f["sw3"]], axis=1)),
        "sw2": _halves(f["sw2"]),
        "sb13": np.concatenate([f["sb1"], f["sb3"]]).reshape(2 * KS, P).T,
    }
    laid = {n: np.ascontiguousarray(v) for n, v in laid.items()}
    nc = bacc.Bacc("TRN2", target_bir_lowering=False, num_devices=1)
    aps = {n: nc.dram_tensor(f"in_{n}", v.shape, mb.dt.from_np(v.dtype), kind="ExternalInput").ap() for n, v in laid.items()}
    out = nc.dram_tensor("out", [OUT_ROWS, D], F32, kind="ExternalOutput").ap()
    build(nc, aps, out)
    r = run_bass_kernel_spmd(nc, [{f"in_{n}": v for n, v in laid.items()}], core_ids=[0])
    return r.results[0]["out"][:TOKENS].reshape(_OUT)
```
